# Optimizing a Trainium2 kernel written in Bass

```python
import numpy as np
import jax
import jax.numpy as jnp

def _softmax(x, axis=-1):
    return jax.nn.softmax(x, axis=axis)
def _gelu(x):
    return jax.nn.gelu(x, approximate=True)
def _silu(x):
    return jax.nn.silu(x)
def _sigmoid(x):
    return jax.nn.sigmoid(x)
def _layernorm(x, axis=-1, eps=1e-5):
    m = jnp.mean(x, axis=axis, keepdims=True)
    v = jnp.var(x, axis=axis, keepdims=True)
    return (x - m) / jnp.sqrt(v + eps)
def _scatter_add(tgt, idx, src, axis=0):
    return tgt.at[idx].add(src)
def _segment_sum(src, seg, n):
    return jax.ops.segment_sum(src, seg, n)

kernel_name = 'mk_conv_attn_hybrid_d2_conv_nchw128_bec5f7'

def setup_inputs(seed: int = 0):
    np.random.seed(seed)
    _w = jnp.asarray
    def _rec_inputs():
        import jax
        import jax.numpy as jnp
        _gk = jax.random.key(seed)
        x = -0.0002928 + 1 * jax.random.normal(jax.random.fold_in(_gk, 1), (32, 128, 32, 32), jnp.float32)
        return x
    x = _rec_inputs()
    def _L0_conv_setup():
        import jax, jax.numpy as jnp
        import numpy as np
        PAD = 1
        key = jax.random.key(seed)
        k1, k2, k3 = jax.random.split(key, 3)
        N, C, F, H, W, HH, WW = (32, 128, 128, 32, 32, 3, 3)
        x = jax.random.normal(k1, (N, C, H, W), dtype=jnp.float32)
        weight = jax.random.normal(k2, (F, C, HH, WW), dtype=jnp.float32) * 0.05
        bias = jax.random.normal(k3, (F,), dtype=jnp.float32) * 0.05
        return {'x': x, 'weight': weight, 'bias': bias}
    _L0_conv_all = _L0_conv_setup()
    _L0_conv_in = {k: v for k, v in _L0_conv_all.items() if k in ('weight', 'bias', )}
    del _L0_conv_all

    def _L1_attn_setup():
        import jax, jax.numpy as jnp
        import numpy as np
        B, S, H, D = (8, 1024, 16, 8)
        E, FFN = (H * D, 512)
        NQ_FFN = 8
        EPS = 1e-05

        def _qz_ring(phi):
            c = jnp.cos(phi)
            P = jnp.cumprod(c, axis=-1)
            z0 = jnp.prod(c[..., 1:], axis=-1, keepdims=True)
            return jnp.concatenate([z0, P[..., 1:]], axis=-1)

        def _ln(v, g, b):
            mu = jnp.mean(v, axis=-1, keepdims=True)
            var = jnp.mean((v - mu) ** 2, axis=-1, keepdims=True)
            return (v - mu) * jax.lax.rsqrt(var + EPS) * g + b
        key = jax.random.key(seed)
        ks = jax.random.split(key, 8)
        inp = {'x': jax.random.normal(ks[0], (B, S, E), jnp.float32), 'rx_theta': jax.random.normal(ks[1], (D,), jnp.float32), 'ry_theta': jax.random.normal(ks[2], (NQ_FFN,), jnp.float32), 'w_comb': jax.random.normal(ks[3], (E, E), jnp.float32) / np.sqrt(E), 'b_comb': jnp.zeros((E,), jnp.float32), 'w1': jax.random.normal(ks[4], (FFN, NQ_FFN), jnp.float32) / np.sqrt(NQ_FFN), 'b1': jnp.zeros((FFN,), jnp.float32), 'w2': jax.random.normal(ks[5], (E, FFN), jnp.float32) / np.sqrt(FFN), 'b2': jnp.zeros((E,), jnp.float32), 'g1': jnp.ones((E,), jnp.float32), 'beta1': jnp.zeros((E,), jnp.float32), 'g2': jnp.ones((E,), jnp.float32), 'beta2': jnp.zeros((E,), jnp.float32)}
        return inp
    _L1_attn_all = _L1_attn_setup()
    _L1_attn_in = {k: v for k, v in _L1_attn_all.items() if k in ('rx_theta', 'ry_theta', 'w_comb', 'b_comb', 'w1', 'b1', 'w2', 'b2', 'g1', 'beta1', 'g2', 'beta2', )}
    del _L1_attn_all

    def _L1_ffn_setup():
        import jax, jax.numpy as jnp
        import numpy as np
        B, N, D, C, E, K = (8, 8192, 128, 128, 8, 2)
        key = jax.random.key(seed)
        k0, k1, k2 = jax.random.split(key, 3)
        x = jax.random.normal(k0, (B, N, D), dtype=jnp.float32)
        router_w = jax.random.normal(k1, (D, E), dtype=jnp.float32) * 0.05
        router_b = jnp.zeros((E,), dtype=jnp.float32)
        expert_w = jax.random.normal(k2, (E, D, C), dtype=jnp.float32) * (1.0 / np.sqrt(D))
        expert_b = jnp.zeros((E, C), dtype=jnp.float32)
        return {'x': x, 'router_w': router_w, 'router_b': router_b, 'expert_w': expert_w, 'expert_b': expert_b}
    _L1_ffn_all = _L1_ffn_setup()
    _L1_ffn_in = {k: v for k, v in _L1_ffn_all.items() if k in ('router_w', 'router_b', 'expert_w', 'expert_b', )}
    del _L1_ffn_all

    return {
        "x": x,
        "L0_conv_weight": _L0_conv_in["weight"],
        "L0_conv_bias": _L0_conv_in["bias"],
        "L1_attn_rx_theta": _L1_attn_in["rx_theta"],
        "L1_attn_ry_theta": _L1_attn_in["ry_theta"],
        "L1_attn_w_comb": _L1_attn_in["w_comb"],
        "L1_attn_b_comb": _L1_attn_in["b_comb"],
        "L1_attn_w1": _L1_attn_in["w1"],
        "L1_attn_b1": _L1_attn_in["b1"],
        "L1_attn_w2": _L1_attn_in["w2"],
        "L1_attn_b2": _L1_attn_in["b2"],
        "L1_attn_g1": _L1_attn_in["g1"],
        "L1_attn_beta1": _L1_attn_in["beta1"],
        "L1_attn_g2": _L1_attn_in["g2"],
        "L1_attn_beta2": _L1_attn_in["beta2"],
        "L1_ffn_router_w": _L1_ffn_in["router_w"],
        "L1_ffn_router_b": _L1_ffn_in["router_b"],
        "L1_ffn_expert_w": _L1_ffn_in["expert_w"],
        "L1_ffn_expert_b": _L1_ffn_in["expert_b"],
    }

def reference(x, L0_conv_weight, L0_conv_bias, L1_attn_rx_theta, L1_attn_ry_theta, L1_attn_w_comb, L1_attn_b_comb, L1_attn_w1, L1_attn_b1, L1_attn_w2, L1_attn_b2, L1_attn_g1, L1_attn_beta1, L1_attn_g2, L1_attn_beta2, L1_ffn_router_w, L1_ffn_router_b, L1_ffn_expert_w, L1_ffn_expert_b):
    import jax
    import jax.numpy as jnp
    def _L0_conv_ref(x, weight, bias):
        import jax, jax.numpy as jnp
        import numpy as np
        PAD = 1
        N, C, H, W = x.shape
        F, _, HH, WW = weight.shape
        pad = PAD
        out_H = H - HH + 1 + 2 * pad
        out_W = W - WW + 1 + 2 * pad
        HHH = max(out_H, HH)
        WWW = max(out_W, WW)
        init_H = H + 2 * pad + HHH - 1
        init_W = W + 2 * pad + WWW - 1
        xp = jnp.pad(x, ((0, 0), (0, 0), (pad, init_H - pad - H), (pad, init_W - pad - W)))
        wp = jnp.pad(weight, ((0, 0), (0, 0), (0, init_H - HH), (0, init_W - WW)))
        xf = jnp.fft.rfft2(xp)
        wf = jnp.fft.rfft2(wp)
        of = jnp.einsum('nchw,fchw->nfhw', xf, jnp.conj(wf))
        out = jnp.fft.irfft2(of, s=(init_H, init_W))[..., :out_H, :out_W]
        return out + bias[None, :, None, None]

    def _L1_attn_ref(x, rx_theta, ry_theta, w_comb, b_comb, w1, b1, w2, b2, g1, beta1, g2, beta2):
        import jax, jax.numpy as jnp
        import numpy as np
        B, S, H, D = (8, 1024, 16, 8)
        E, FFN = (H * D, 512)
        NQ_FFN = 8
        EPS = 1e-05

        def _qz_ring(phi):
            c = jnp.cos(phi)
            P = jnp.cumprod(c, axis=-1)
            z0 = jnp.prod(c[..., 1:], axis=-1, keepdims=True)
            return jnp.concatenate([z0, P[..., 1:]], axis=-1)

        def _ln(v, g, b):
            mu = jnp.mean(v, axis=-1, keepdims=True)
            var = jnp.mean((v - mu) ** 2, axis=-1, keepdims=True)
            return (v - mu) * jax.lax.rsqrt(var + EPS) * g + b
        Bs, Ss, Es = x.shape
        heads = x.reshape(Bs, Ss, H, D)
        qkv = _qz_ring(heads + rx_theta)
        q = jnp.transpose(qkv, (0, 2, 1, 3))
        scores = jnp.einsum('bhsd,bhtd->bhst', q, q) / np.sqrt(D)
        attn = jax.nn.softmax(scores, axis=-1)
        ctx = jnp.einsum('bhst,bhtd->bhsd', attn, q)
        ctx = jnp.transpose(ctx, (0, 2, 1, 3)).reshape(Bs, Ss, Es)
        attn_out = ctx @ w_comb.T + b_comb
        x1 = _ln(x + attn_out, g1, beta1)
        zf = jnp.cos(x1[..., :NQ_FFN]) * jnp.cos(ry_theta)
        h = jax.nn.relu(zf @ w1.T + b1)
        ffn_out = h @ w2.T + b2
        return _ln(x1 + ffn_out, g2, beta2)

    def _L1_ffn_ref(x, router_w, router_b, expert_w, expert_b):
        import jax, jax.numpy as jnp
        import numpy as np
        B, N, D, C, E, K = (8, 8192, 128, 128, 8, 2)
        router_probs = jax.nn.softmax(x @ router_w + router_b, axis=-1)
        top_p, top_i = jax.lax.top_k(router_probs, K)
        top_p = top_p / jnp.sum(top_p, axis=-1, keepdims=True)
        expert_out = jnp.einsum('bnd,edc->bnec', x, expert_w) + expert_b
        gathered = jnp.take_along_axis(expert_out, top_i[..., None], axis=2)
        return jnp.einsum('bnk,bnkc->bnc', top_p, gathered)

    def _gn(v, G=32, eps=1e-5):
        B_, C_, H_, W_ = v.shape
        g = v.reshape(B_, G, C_ // G, H_, W_)
        m = jnp.mean(g, axis=(2, 3, 4), keepdims=True)
        s = jnp.var(g, axis=(2, 3, 4), keepdims=True)
        return ((g - m) / jnp.sqrt(s + eps)).reshape(v.shape)

    def _ln_c(v, eps=1e-6):
        m = jnp.mean(v, axis=1, keepdims=True)
        s = jnp.var(v, axis=1, keepdims=True)
        return (v - m) / jnp.sqrt(s + eps)

    def _ln_t(v, eps=1e-5):
        m = jnp.mean(v, axis=-1, keepdims=True)
        s = jnp.var(v, axis=-1, keepdims=True)
        return (v - m) / jnp.sqrt(s + eps)

    def _to_tokens(v):
        B_, C_, H_, W_ = v.shape
        return v.reshape(B_, C_, H_ * W_).transpose(0, 2, 1)
    def _from_tokens(t, like):
        B_, C_, H_, W_ = like.shape
        return t.transpose(0, 2, 1).reshape(B_, C_, H_, W_)

    x = x + _L0_conv_ref(_gn(x), L0_conv_weight, L0_conv_bias)
    t = _to_tokens(x)
    t = t + _L1_attn_ref(_ln_t(t), L1_attn_rx_theta, L1_attn_ry_theta, L1_attn_w_comb, L1_attn_b_comb, L1_attn_w1, L1_attn_b1, L1_attn_w2, L1_attn_b2, L1_attn_g1, L1_attn_beta1, L1_attn_g2, L1_attn_beta2)
    t = t + _L1_ffn_ref(_ln_t(t), L1_ffn_router_w, L1_ffn_router_b, L1_ffn_expert_w, L1_ffn_expert_b)
    x = _from_tokens(t, x)
    return x


_drawn_inputs = setup_inputs


def setup_inputs(seed=0):
    import zlib

    import numpy as np

    out = dict(_drawn_inputs(seed))
    spreads = {'L1_attn_b_comb': (0.0, 0.1),
     'L1_attn_b1': (0.0, 0.1),
     'L1_attn_b2': (0.0, 0.1),
     'L1_attn_g1': (1.0, 0.2),
     'L1_attn_beta1': (0.0, 0.1),
     'L1_attn_g2': (1.0, 0.2),
     'L1_attn_beta2': (0.0, 0.1),
     'L1_ffn_router_b': (0.0, 0.1),
     'L1_ffn_expert_b': (0.0, 0.336)}
    factors = {}
    for name, (base, spread) in spreads.items():
        noise = np.random.default_rng([zlib.crc32(name.encode()), seed]).standard_normal(out[name].shape)
        drawn = base * np.exp(spread * noise) if base else spread * noise
        out[name] = jnp.asarray(drawn.astype(out[name].dtype))
    for name, factor in factors.items():
        out[name] = (out[name] * factor).astype(out[name].dtype)
    return out
```

```python
import math
from contextlib import ExitStack

import numpy as np
import concourse.bass as bass
from concourse import mybir

F32 = mybir.dt.float32
F16 = mybir.dt.float16
ALU = mybir.AluOpType
ACT = mybir.ActivationFunctionType
AX = mybir.AxisListType

IMAGES, C, SIDE, TOKENS = 32, 128, 32, 1024
PADDED = SIDE + 2
GROUP_CHANNELS = 4
BLOCKS = TOKENS // 128
HALF = TOKENS // 2
HEADS, D = 16, 8
QUADS = HEADS // 4
FEATURES, HIDDEN, CHUNKS = 8, 512, 4
EXPERTS, CHOSEN = 8, 2
GROUPS = QUADS * 2 * BLOCKS
PAIRS = 2 * GROUPS
RING = 4
STRIP = 32
SPLIT = 1024.0
SCORE_SCALE = 1.0 / (math.sqrt(D) * SPLIT * SPLIT)
ROUND = 1.5 * 2.0 ** 23
TURN_HI = 6.28125
TURN_LO = 2.0 * math.pi - 6.28125
SINE_END = 3.1415925
EPS = 1e-5


def schedule():
    jobs = [(2, "attend", "key", 3, 0), (2, "attend", "key", 3, 1)]
    jobs += [(i, "finish", "context", i, 0) for i in range(BLOCKS)]
    jobs += [(3, "prepare", "mean", 0, 0), (5, "prepare", "spread", 0, 0)]
    jobs += [(8 + i, "finish", "turn_context", i, 0) for i in range(2)]
    jobs += [(10 + i, "finish", "combine", i, 0) for i in range(2)]
    jobs += [(12 + 3 * i + j, "prepare", "conv", i, j) for i in range(2) for j in range(3)]
    jobs += [(18 + i, "prepare", "tokens", i, 0) for i in range(2)]
    jobs += [(33 + i, "finish", "features", i, 0) for i in range(2)]
    jobs += [(35 + 2 * i + j // 2, "finish", "hidden", i, j) for i in range(2) for j in range(CHUNKS)]
    jobs += [(39 + i, "finish", "project", i, 0) for i in range(2)]
    jobs += [(42 + 2 * h + v, "prepare", "key", h, v) for h in range(2) for v in range(2)]
    jobs += [(49, "prepare", "key", 2, v) for v in range(2)]
    jobs += [(50 + i, "finish", "turn_tokens", i, 0) for i in range(2)]
    jobs += [(52, "finish", "route", i, 0) for i in range(2)]
    jobs += [(55, "finish", "turn_gates", i, 0) for i in range(2)]
    jobs += [(56, "finish", "expert_bias", i, 0) for i in range(2)]
    jobs += [(57 + i * 2 // 3, "finish", "expert", i, j) for i in range(BLOCKS) for j in range(2)]
    jobs += [(63, "finish", "image", i, 0) for i in range(2)]
    return sorted(jobs, key=lambda job: job[0])


JOBS = schedule()
LAST_TAPS = 2


def numbered(stages):
    out, number = [], 0
    for group, stage, kind, i, j in JOBS:
        if stage in stages:
            out.append((group, kind, i, j, number))
            number += not (kind == "conv" and j < LAST_TAPS)
    return out, number


STEADY = ("attend", "prepare", "finish")


def stages_of(b):
    if not isinstance(b, int):
        return STEADY
    return (("attend",) if 0 <= b < IMAGES else ()) + (("prepare",) if b + 1 < IMAGES else ()) \
        + (("finish",) if b >= 1 else ())


def before(b, count):
    if isinstance(b, int):
        return sum(count(stages_of(s)) for s in range(-1, b))
    first = count(stages_of(-1)) + count(stages_of(0))
    return (b - 1) * count(STEADY) + first


def conv_hybrid(nc, x, conv_w, conv_b, group_mean, identity, theta, ry, w_comb, b_comb, w1, b1, w2, b2,
                g1, beta1, g2, beta2, router_w, router_b, expert_w, expert_b, earlier, out):
    ctx = ExitStack()
    with ctx:
        def sb(name, shape, dtype=F32):
            return ctx.enter_context(nc.sbuf_tensor(name, shape, dtype))

        def sem(name):
            return ctx.enter_context(nc.semaphore(name))

        w_conv = sb("w_conv", [C, 9, C])
        bias_conv = sb("bias_conv", [C, 1])
        mean_of_group = sb("mean_of_group", [C, C])
        ident = sb("ident", [128, 128])
        ident16 = sb("ident16", [128, 128], F16)
        shift = sb("shift", [128, C])
        ry_angle = sb("ry_angle", [128, 3, FEATURES])
        cos_ry = sb("cos_ry", [128, FEATURES])
        w_combine = sb("w_combine", [C, C])
        bias_combine = sb("bias_combine", [128, C])
        w_hidden = sb("w_hidden", [FEATURES, HIDDEN])
        bias_hidden = sb("bias_hidden", [128, CHUNKS])
        w_project = sb("w_project", [128, CHUNKS, C])
        bias_project = sb("bias_project", [128, C])
        gain1 = sb("gain1", [128, C])
        offset1 = sb("offset1", [128, C])
        gain2 = sb("gain2", [128, C])
        offset2 = sb("offset2", [128, C])
        w_router = sb("w_router", [C, EXPERTS])
        bias_router = sb("bias_router", [128, EXPERTS])
        w_expert = sb("w_expert", [C, EXPERTS * C])
        bias_expert = sb("bias_expert", [EXPERTS, C])
        is_earlier = sb("is_earlier", [128, EXPERTS, EXPERTS])
        minus_half = sb("minus_half", [128, BLOCKS])
        eps = sb("eps", [128, BLOCKS])

        image = sb("image", [C, TOKENS])
        pixel_stats = sb("pixel_stats", [C, 2, 6])
        channel_stats = sb("channel_stats", [C, 2])
        group_stats = sb("group_stats", [C, 4])
        group_rstd = sb("group_rstd", [C, 2])
        padded = sb("padded", [C, PADDED, PADDED])
        layer0 = sb("layer0", [C, TOKENS])
        tokens_new = sb("tokens_new", [128, BLOCKS, C])
        normed_new = sb("normed_new", [128, BLOCKS, C])
        scratch = sb("scratch", [128, CHUNKS, TOKENS])
        angle, turns = (scratch[:, n, :].rearrange("p (a c) -> p a c", a=BLOCKS) for n in range(2))
        cosine = scratch[:, 2, :].rearrange("p (h d) -> p h d", d=D)
        product = sb("product", [128, BLOCKS * HEADS, D])
        key_halves = sb("key_halves", [128, BLOCKS, HEADS, 4 * D], F16)
        query_halves = sb("query_halves", [128, BLOCKS, HEADS, 4 * D], F16)

        keys = sb("keys", [128, QUADS, TOKENS], F16)
        queries = sb("queries", [128, QUADS, TOKENS], F16)
        values = sb("values", [128, BLOCKS, HEADS, STRIP])
        probs = sb("probs", [128, RING, 2 * HALF])
        sums = sb("sums", [128, QUADS, TOKENS])

        tokens_mid = sb("tokens_mid", [128, BLOCKS, C])
        tokens_old = sb("tokens_old", [128, BLOCKS, C])
        normed_old = sb("normed_old", [128, BLOCKS, C])
        weight_inv = sb("weight_inv", [128, 2, HEADS])
        context = sb("context", [128, BLOCKS, C])
        context_t = sb("context_t", [C, TOKENS])
        attended = sb("attended", [128, BLOCKS, C])
        normed1 = sb("normed1", [128, BLOCKS, C])
        x1 = sb("x1", [128, BLOCKS, C])
        x1_bias = sb("x1_bias", [128, BLOCKS, C])
        feature_angle = sb("feature_angle", [128, BLOCKS, FEATURES])
        feature_turns = sb("feature_turns", [128, BLOCKS, FEATURES])
        feature_cos = sb("feature_cos", [128, BLOCKS, FEATURES])
        feature = sb("feature", [128, BLOCKS, FEATURES])
        feature_t = sb("feature_t", [FEATURES, TOKENS])
        hidden = scratch
        projected = attended
        normed2 = sb("normed2", [128, BLOCKS, C])
        x2 = sb("x2", [128, BLOCKS, C])
        normed3, normed3_t = context, context_t
        logits = sb("logits", [128, BLOCKS, EXPERTS])
        top = sb("top", [128, BLOCKS])
        below = sb("below", [128, BLOCKS, EXPERTS])
        ahead_of = sb("ahead_of", [128, BLOCKS, EXPERTS, EXPERTS])
        tied = sb("tied", [128, BLOCKS, EXPERTS, EXPERTS])
        rank = sb("rank", [128, BLOCKS, EXPERTS])
        weight = sb("weight", [128, BLOCKS, EXPERTS])
        chosen = sb("chosen", [128, BLOCKS, EXPERTS])
        chosen_sum = sb("chosen_sum", [128, BLOCKS])
        chosen_inv = sb("chosen_inv", [128, BLOCKS])
        gates = sb("gates", [128, BLOCKS, EXPERTS])
        gates_t = sb("gates_t", [EXPERTS, TOKENS])
        mixed = x2
        image_out = sb("image_out", [C, TOKENS])
        block_stats = sb("block_stats", [128, BLOCKS, 6])
        token_stats = sb("token_stats", [128, BLOCKS, 2])
        variance = sb("variance", [128, BLOCKS])
        rstd = sb("rstd", [128, BLOCKS])

        scores = [ctx.enter_context(nc.psum_tensor(f"scores{n}", [128, 2 * HALF], F32)) for n in range(2)]
        sums_acc = ctx.enter_context(nc.psum_tensor("sums_acc", [128, 2, HALF], F32))
        bank = [ctx.enter_context(nc.psum_tensor(f"bank{n}", [128, HALF], F32)) for n in range(2)]

        weights_loaded = sem("weights_loaded")
        image_loaded = sem("image_loaded")
        filled = sem("filled")
        ry_reduced, ry_cosine = sem("ry_reduced"), sem("ry_cosine")
        job_ready = sem("job_ready")
        job_taken = sem("job_taken")
        scores_ready = sem("scores_ready")
        probs_ready = sem("probs_ready")
        probs_used = sem("probs_used")
        sums_saved = sem("sums_saved")
        head_ready = sem("head_ready")
        moments_ready = sem("moments_ready")
        deviation_ready = sem("deviation_ready")
        group_rstd_ready = sem("group_rstd_ready")
        padded_ready = sem("padded_ready")
        stats_ready = sem("stats_ready")
        rstd_ready = sem("rstd_ready")
        moved_on = sem("moved_on")
        normed_ready = sem("normed_ready")
        angle_ready, cosine_ready = sem("angle_ready"), sem("cosine_ready")
        feature_angle_ready, feature_cos_ready = sem("feature_angle_ready"), sem("feature_cos_ready")
        halves_ready = sem("halves_ready")
        normed1_ready, x1_ready = sem("normed1_ready"), sem("x1_ready")
        normed2_ready, x2_ready = sem("normed2_ready"), sem("x2_ready")
        x1_bias_ready = sem("x1_bias_ready")
        feature_ready = sem("feature_ready")
        normed3_ready = sem("normed3_ready")
        below_ready, weight_ready = sem("below_ready"), sem("weight_ready")
        gates_ready = sem("gates_ready")
        image_stored = sem("image_stored")
        vector_step = sem("vector_step")
        pool_step = sem("pool_step")

        loads = [(w_conv, conv_w), (bias_conv, conv_b), (mean_of_group, group_mean), (ident, identity),
                 (shift, theta), (ry_angle[:, 0, :], ry), (w_combine, w_comb), (bias_combine, b_comb),
                 (w_hidden, w1), (bias_hidden, b1), (w_project, w2), (bias_project, b2), (gain1, g1),
                 (offset1, beta1), (gain2, g2), (offset2, beta2), (w_router, router_w),
                 (bias_router, router_b), (w_expert, expert_w), (bias_expert, expert_b),
                 (is_earlier, earlier)]
        FILLS = 6

        def everywhere(row):
            return row[:, :].unsqueeze(1).broadcast_to([128, BLOCKS, row.shape[1]])

        def finishes(b):
            return before(b, lambda stages: int("finish" in stages))

        def job_counter(b):
            jobs, _ = numbered(stages_of(b))
            base = before(b, lambda stages: numbered(stages)[1])
            where = {(kind, i, j): number for _, kind, i, j, number in jobs}
            return jobs, base, where

        def wait(engine, semaphore, value):
            if not isinstance(value, int) or value > 0:
                engine.wait_ge(semaphore, value)

        def steps(engine, body):
            body(-1)
            body(0)
            with engine.Fori(1, IMAGES - 1) as b:
                body(b)
            body(IMAGES - 1)
            body(IMAGES)

        block = ctx.enter_context(nc.Block())

        @block.sync
        def _(sp):
            for tile, source in loads:
                sp.dma_start(tile if isinstance(tile, bass.AP) else tile[:], source).then_inc(weights_loaded, 16)

            def step(b):
                stages = stages_of(b)
                jobs, base, where = job_counter(b)
                if "prepare" in stages:
                    wait(sp, angle_ready, b + 1)
                    sp.dma_start(image[:], x[b + 1, :, :]).then_inc(image_loaded, 16)
                if "finish" in stages:
                    wait(sp, job_taken, base + where["image", 1, 0] + 1)
                    sp.dma_start(out[b - 1, :, :], image_out[:]).then_inc(image_stored, 16)

            steps(sp, step)
            sp.wait_ge(image_stored, 16 * IMAGES)

        @block.tensor
        def _(pe):
            pe.wait_ge(weights_loaded, 16 * len(loads))
            pe.wait_ge(filled, FILLS)

            def score_pair(b, group, pair):
                quad, half, blk = group // 16, group // 8 % 2, group % 8
                wait(pe, probs_ready, b * PAIRS + 2 * group + pair - 1)
                for n in range(2):
                    head = 2 * pair + n
                    rows = slice(STRIP * head, STRIP * (head + 1))
                    last = nc.tensor.matmul(scores[pair][:, n * HALF:(n + 1) * HALF],
                                            keys[rows, quad, 128 * blk:128 * (blk + 1)],
                                            queries[rows, quad, half * HALF:(half + 1) * HALF],
                                            start=True, stop=True)
                last.then_inc(scores_ready, 1)

            def first_scores(b):
                pe.wait_ge(head_ready, b * QUADS + 1)
                score_pair(b, 0, 0)
                score_pair(b, 0, 1)

            def sum_group(b, group):
                quad, half, blk = group // 16, group // 8 % 2, group % 8
                unit = 2 * quad + half
                if blk == 0:
                    wait(pe, sums_saved, b * 2 * QUADS + unit - 1)
                pe.wait_ge(probs_ready, b * PAIRS + 2 * group + 2)
                for head in range(4):
                    pair = 2 * group + head // 2
                    last = nc.tensor.matmul(sums_acc[STRIP * head:STRIP * (head + 1), half, :],
                                            values[:, blk, 4 * quad + head, :],
                                            probs[:, pair % RING, (head % 2) * HALF:(head % 2 + 1) * HALF],
                                            start=(blk == 0), stop=(blk == BLOCKS - 1))
                last.then_inc(probs_used, 1)

            def job(b, base, where, kind, i, j, number):
                to = bank[number % 2]

                def taken(*which):
                    pe.wait_ge(job_taken, base + where[which] + 1)

                if kind != "conv" or j == 0:
                    wait(pe, job_taken, base + number - 1)
                if kind == "mean":
                    pe.wait_ge(moments_ready, b + 2)
                    last = nc.tensor.matmul(to[:, 0:1], mean_of_group[:], channel_stats[:, 0:1], start=True, stop=True)
                elif kind == "spread":
                    pe.wait_ge(deviation_ready, b + 2)
                    last = nc.tensor.matmul(to[:, 0:1], mean_of_group[:], group_stats[:, 2:3], start=True, stop=True)
                elif kind == "conv":
                    if j == 0:
                        pe.wait_ge(padded_ready, b + 2)
                    for tap in range(3 * j, 3 * j + 3):
                        row = i * SIDE // 2 + tap // 3
                        last = nc.tensor.matmul(to[:, :], w_conv[:, tap, :],
                                                padded[:, row:row + SIDE // 2, tap % 3:tap % 3 + SIDE],
                                                start=(tap == 0), stop=(tap == 8))
                elif kind in ("tokens", "turn_context", "turn_tokens", "image"):
                    if kind == "tokens":
                        taken("conv", i, LAST_TAPS)
                    elif kind == "turn_context":
                        taken("context", 4 * i + 3, 0)
                    elif kind == "turn_tokens":
                        pe.wait_ge(normed3_ready, finishes(b) + 1)
                    else:
                        taken("expert", 4 * i + 3, 1)
                    source = {"turn_context": context, "turn_tokens": normed3, "image": mixed}
                    for n in range(4):
                        blk = 4 * i + n
                        piece = layer0[:, 128 * blk:128 * (blk + 1)] if kind == "tokens" else source[kind][:, blk, :]
                        last = nc.tensor.transpose(to[:, 128 * n:128 * (n + 1)], piece, ident[:])
                elif kind == "key":
                    of_next = 0 if i == QUADS - 1 else 1
                    pe.wait_ge(halves_ready, b + 1 + of_next)
                    for blk in range(BLOCKS):
                        piece = (query_halves if j else key_halves)[:, blk, 4 * i:4 * i + 4, :]
                        last = nc.tensor.transpose(to[:, :].bitcast(F16)[:, 128 * blk:128 * (blk + 1)],
                                                   piece.rearrange("p h d -> p (h d)"), ident16[:])
                elif kind == "context":
                    if i == 0:
                        pe.wait_ge(sums_saved, b * 2 * QUADS)
                    for quad in range(QUADS):
                        last = nc.tensor.transpose(to[:, 128 * quad:128 * (quad + 1)],
                                                   sums[:, quad, 128 * i:128 * (i + 1)], ident[:])
                elif kind == "combine":
                    taken("turn_context", i, 0)
                    for n in range(4):
                        last = nc.tensor.matmul(to[:, 128 * n:128 * (n + 1)],
                                                context_t[:, 128 * (4 * i + n):128 * (4 * i + n + 1)],
                                                w_combine[:], start=True, stop=True)
                elif kind in ("features", "turn_gates"):
                    pe.wait_ge(feature_ready if kind == "features" else gates_ready, finishes(b) + 1)
                    source = feature if kind == "features" else gates
                    for n in range(4):
                        last = nc.tensor.transpose(to[0:FEATURES, 128 * n:128 * (n + 1)],
                                                   source[:, 4 * i + n, :], ident[:])
                elif kind == "hidden":
                    taken("features", i, 0)
                    last = nc.tensor.matmul(to[:, :], w_hidden[:, 128 * j:128 * (j + 1)],
                                            feature_t[:, i * HALF:(i + 1) * HALF], start=True, stop=True)
                elif kind == "project":
                    taken("hidden", i, CHUNKS - 1)
                    for n in range(4):
                        at = 128 * (4 * i + n)
                        for chunk in range(CHUNKS):
                            last = nc.tensor.matmul(to[:, 128 * n:128 * (n + 1)], hidden[:, chunk, at:at + 128],
                                                    w_project[:, chunk, :],
                                                    start=(chunk == 0), stop=(chunk == CHUNKS - 1))
                elif kind == "route":
                    taken("turn_tokens", i, 0)
                    for n in range(4):
                        last = nc.tensor.matmul(to[:, EXPERTS * n:EXPERTS * (n + 1)],
                                                normed3_t[:, 128 * (4 * i + n):128 * (4 * i + n + 1)],
                                                w_router[:], start=True, stop=True)
                elif kind == "expert_bias":
                    taken("turn_gates", i, 0)
                    for n in range(4):
                        last = nc.tensor.matmul(to[:, 128 * n:128 * (n + 1)],
                                                gates_t[:, 128 * (4 * i + n):128 * (4 * i + n + 1)],
                                                bias_expert[:], start=True, stop=True)
                elif kind == "expert":
                    last = nc.tensor.matmul(to[:, :], normed3_t[:, 128 * i:128 * (i + 1)],
                                            w_expert[:, j * HALF:(j + 1) * HALF], start=True, stop=True)
                if kind != "conv" or j == LAST_TAPS:
                    last.then_inc(job_ready, 1)

            def step(b):
                stages = stages_of(b)
                jobs, base, where = job_counter(b)
                for group in range(GROUPS):
                    if "attend" in stages:
                        if group + 1 < GROUPS:
                            if (group + 1) % 16 == 0:
                                pe.wait_ge(head_ready, b * QUADS + (group + 1) // 16 + 1)
                            score_pair(b, group + 1, 0)
                            score_pair(b, group + 1, 1)
                        sum_group(b, group)
                    for at, kind, i, j, number in jobs:
                        if at == group:
                            job(b, base, where, kind, i, j, number)
                if "prepare" in stages:
                    first_scores(b + 1)

            steps(pe, step)

        @block.scalar
        def _(act):
            act.wait_ge(ry_reduced, 1)
            nc.scalar.activation(cos_ry[:], ry_angle[:, 2, :], ACT.Sin).then_inc(ry_cosine, 1)

            def sines(b, stages):
                if "finish" in stages:
                    act.wait_ge(feature_angle_ready, finishes(b) + 1)
                    nc.scalar.activation(feature_cos[:], feature_angle[:], ACT.Sin).then_inc(feature_cos_ready, 1)
                if "prepare" in stages:
                    act.wait_ge(angle_ready, b + 2)
                    nc.scalar.activation(cosine[:].rearrange("p a d -> p (a d)"),
                                         angle[:].rearrange("p a d -> p (a d)"), ACT.Sin).then_inc(cosine_ready, 1)

            def gate_exponentials(b):
                act.wait_ge(below_ready, finishes(b) + 1)
                nc.scalar.activation(weight[:], below[:], ACT.Exp).then_inc(weight_ready, 1)

            def step(b):
                stages = stages_of(b)
                for pair in range(PAIRS):
                    if "attend" in stages:
                        act.wait_ge(scores_ready, b * PAIRS + pair + 1)
                        if pair % 2 == 0:
                            wait(act, probs_used, b * GROUPS + pair // 2 - RING // 2 + 1)
                        nc.scalar.activation(probs[:, pair % RING, :], scores[pair % 2][:, :], ACT.Exp,
                                             scale=SCORE_SCALE).then_inc(probs_ready, 1)
                    if pair == 2 * 30:
                        sines(b, stages)
                    if pair == 2 * 54 and "finish" in stages:
                        gate_exponentials(b)

            steps(act, step)

        @block.gpsimd
        def _(pool):
            nc.gpsimd.memset(minus_half[:], -0.5).then_inc(filled, 1)
            nc.gpsimd.memset(eps[:], EPS).then_inc(filled, 1)
            nc.gpsimd.memset(padded[:], 0.0).then_inc(filled, 1)
            pool.wait_ge(filled, FILLS)
            pool.wait_ge(weights_loaded, 16 * len(loads))
            done = [0]

            def link(instruction):
                instruction.then_inc(pool_step, 1)
                done[0] += 1
                pool.wait_ge(pool_step, done[0])

            def layer_rstd(b, n):
                base = before(b, lambda stages: ("prepare" in stages) + 3 * ("finish" in stages))
                pool.wait_ge(stats_ready, base + n + 1)
                link(nc.gpsimd.tensor_tensor(variance[:], token_stats[:, :, 1], eps[:], ALU.add))
                nc.gpsimd.tensor_tensor(rstd[:], variance[:], minus_half[:], ALU.pow).then_inc(rstd_ready, 1)

            def step(b):
                stages = stages_of(b)
                jobs, base, where = job_counter(b)
                done[0] = 0
                n = 0
                if "prepare" in stages:
                    pool.wait_ge(job_taken, base + where["spread", 0, 0] + 1)
                    link(nc.gpsimd.tensor_tensor(group_rstd[:, 0:1], group_stats[:, 3:4], eps[:, 0:1], ALU.add))
                    nc.gpsimd.tensor_tensor(group_rstd[:, 1:2], group_rstd[:, 0:1], minus_half[:, 0:1],
                                            ALU.pow).then_inc(group_rstd_ready, 1)
                if "finish" in stages:
                    layer_rstd(b, n)
                    n += 1
                    link(nc.gpsimd.tensor_tensor(tokens_old[:], tokens_mid[:], everywhere(offset2), ALU.add))
                if "attend" in stages:
                    wait(pool, normed_ready, b + 1)
                    nc.gpsimd.tensor_tensor(normed_old[:], normed_new[:], everywhere(bias_combine), ALU.add)
                    nc.gpsimd.tensor_copy(tokens_mid[:], tokens_new[:]).then_inc(moved_on, 1)
                if "finish" in stages:
                    pool.wait_ge(normed1_ready, finishes(b) + 1)
                    link(nc.gpsimd.tensor_tensor(normed1[:], normed1[:], everywhere(gain1), ALU.mult))
                    nc.gpsimd.tensor_tensor(x1[:], normed1[:], everywhere(offset1), ALU.add).then_inc(x1_ready, 1)
                    pool.wait_ge(x1_ready, finishes(b) + 1)
                    nc.gpsimd.tensor_tensor(x1_bias[:], x1[:], everywhere(bias_project),
                                            ALU.add).then_inc(x1_bias_ready, 1)
                if "prepare" in stages:
                    layer_rstd(b, n)
                    n += 1
                if "finish" in stages:
                    layer_rstd(b, n)
                    n += 1
                    pool.wait_ge(normed2_ready, finishes(b) + 1)
                    link(nc.gpsimd.tensor_tensor(normed2[:], normed2[:], everywhere(gain2), ALU.mult))
                    nc.gpsimd.tensor_tensor(x2[:], normed2[:], tokens_old[:], ALU.add).then_inc(x2_ready, 1)
                    layer_rstd(b, n)
                pool.sem_clear(pool_step)

            steps(pool, step)

        @block.vector
        def _(dve):
            done = [0]

            def link(instruction):
                instruction.then_inc(vector_step, 1)
                done[0] += 1
                dve.wait_ge(vector_step, done[0])

            def reduce_angle(a, t):
                link(nc.vector.tensor_scalar(t, a, 1.0 / (2.0 * math.pi), ROUND, ALU.mult, ALU.add))
                link(nc.vector.tensor_scalar(t, t, ROUND, None, ALU.subtract))
                link(nc.vector.scalar_tensor_tensor(a, t, -TURN_HI, a, ALU.mult, ALU.add))
                link(nc.vector.scalar_tensor_tensor(a, t, -TURN_LO, a, ALU.mult, ALU.add))
                return nc.vector.tensor_scalar(a, a, SINE_END, -SINE_END, ALU.min, ALU.max)

            nc.vector.memset(values[:, :, :, D + 1:STRIP], 0.0).then_inc(filled, 1)
            nc.vector.memset(values[:, :, :, D:D + 1], 1.0).then_inc(filled, 1)
            dve.wait_ge(weights_loaded, 16 * len(loads))
            nc.vector.tensor_copy(ident16[:], ident[:]).then_inc(filled, 1)
            link(nc.vector.tensor_scalar(shift[:], shift[:], math.pi / 2.0, None, ALU.add))
            link(nc.vector.tensor_scalar(ry_angle[:, 2, :], ry_angle[:, 0, :], math.pi / 2.0, None, ALU.add))
            reduce_angle(ry_angle[:, 2, :], ry_angle[:, 1, :]).then_inc(ry_reduced, 1)
            dve.wait_ge(filled, FILLS)
            dve.wait_ge(ry_cosine, 1)
            dve.sem_clear(vector_step)

            def channel_moments(b):
                dve.wait_ge(image_loaded, 16 * (b + 2))
                nc.vector.bn_stats(pixel_stats[:, 0, :], image[:, 0:HALF])
                link(nc.vector.bn_stats(pixel_stats[:, 1, :], image[:, HALF:TOKENS]))
                nc.vector.bn_aggr(channel_stats[:], pixel_stats[:].rearrange("p a s -> p (a s)")).then_inc(moments_ready, 1)

            def normalise_image(b):
                dve.wait_ge(group_rstd_ready, b + 2)
                nc.vector.tensor_scalar(padded[:, 1:SIDE + 1, 1:SIDE + 1],
                                        image[:].rearrange("p (r c) -> p r c", c=SIDE),
                                        group_stats[:, 0:1], group_rstd[:, 1:2],
                                        ALU.subtract, ALU.mult).then_inc(padded_ready, 1)

            def layer_norm(b, n, source, target):
                base = before(b, lambda stages: ("prepare" in stages) + 3 * ("finish" in stages))
                for blk in range(BLOCKS - 1):
                    nc.vector.bn_stats(block_stats[:, blk, :], source[:, blk, :])
                link(nc.vector.bn_stats(block_stats[:, BLOCKS - 1, :], source[:, BLOCKS - 1, :]))
                for blk in range(BLOCKS):
                    last = nc.vector.bn_aggr(token_stats[:, blk, :], block_stats[:, blk, :])
                last.then_inc(stats_ready, 1)
                dve.wait_ge(rstd_ready, base + n + 1)
                for blk in range(BLOCKS):
                    last = nc.vector.tensor_scalar(target[:, blk, :], source[:, blk, :], token_stats[:, blk, 0:1],
                                                   rstd[:, blk:blk + 1], ALU.subtract, ALU.mult)
                return last

            def cosine_products(b):
                dve.wait_ge(cosine_ready, b + 2)
                cos = [cosine[:, :, d] for d in range(D)]
                nc.vector.tensor_tensor(product[:, :, 0], cos[1], cos[2], ALU.mult)
                link(nc.vector.tensor_tensor(product[:, :, 1], cos[0], cos[1], ALU.mult))
                for d in range(2, D):
                    if d + 1 < D:
                        nc.vector.tensor_tensor(product[:, :, 0], product[:, :, 0], cos[d + 1], ALU.mult)
                    link(nc.vector.tensor_tensor(product[:, :, d], product[:, :, d - 1], cos[d], ALU.mult))
                as_keys = key_halves[:].rearrange("p a h (r d) -> p (a h) r d", r=4)
                as_queries = query_halves[:].rearrange("p a h (r d) -> p (a h) r d", r=4)
                link(nc.vector.tensor_scalar(as_keys[:, :, 0, :], product[:], SPLIT, None, ALU.mult))
                link(nc.vector.scalar_tensor_tensor(as_keys[:, :, 1, :], product[:], SPLIT, as_keys[:, :, 0, :],
                                                    ALU.mult, ALU.subtract))
                nc.vector.tensor_copy(as_keys[:, :, 2:4, :], as_keys[:, :, 0:2, :])
                nc.vector.tensor_copy(as_queries[:, :, 0:2, :], as_keys[:, :, 0:2, :])
                nc.vector.tensor_copy(as_queries[:, :, 2, :], as_keys[:, :, 1, :])
                nc.vector.tensor_copy(as_queries[:, :, 3, :], as_keys[:, :, 0, :]).then_inc(halves_ready, 1)

            def pick_experts(b):
                gate_shape = [128, BLOCKS, EXPERTS]
                all_pairs = [128, BLOCKS, EXPERTS, EXPERTS]
                link(nc.vector.tensor_reduce(top[:], logits[:], axis=AX.X, op=ALU.max))
                nc.vector.tensor_tensor(below[:], logits[:], top[:].unsqueeze(2).broadcast_to(gate_shape),
                                        ALU.subtract).then_inc(below_ready, 1)
                other, own = (logits[:].unsqueeze(2).broadcast_to(all_pairs),
                              logits[:].unsqueeze(3).broadcast_to(all_pairs))
                nc.vector.tensor_tensor(ahead_of[:], other, own, ALU.is_gt)
                link(nc.vector.tensor_tensor(tied[:], other, own, ALU.is_equal))
                link(nc.vector.tensor_tensor(tied[:], tied[:], is_earlier[:].unsqueeze(1).broadcast_to(all_pairs),
                                             ALU.mult))
                link(nc.vector.tensor_tensor(ahead_of[:], ahead_of[:], tied[:], ALU.add))
                link(nc.vector.tensor_reduce(rank[:], ahead_of[:], axis=AX.X, op=ALU.add))
                dve.wait_ge(weight_ready, finishes(b) + 1)
                link(nc.vector.scalar_tensor_tensor(chosen[:], rank[:], float(CHOSEN), weight[:], ALU.is_lt, ALU.mult))
                link(nc.vector.tensor_reduce(chosen_sum[:], chosen[:], axis=AX.X, op=ALU.add))
                link(nc.vector.reciprocal(chosen_inv[:], chosen_sum[:]))
                nc.vector.tensor_tensor(gates[:], chosen[:], chosen_inv[:].unsqueeze(2).broadcast_to(gate_shape),
                                        ALU.mult).then_inc(gates_ready, 1)

            def save_sums(b, unit):
                quad, half = unit // 2, unit % 2
                dve.wait_ge(probs_used, b * GROUPS + BLOCKS * (unit + 1))
                nc.vector.tensor_copy(sums[:, quad, half * HALF:(half + 1) * HALF],
                                      sums_acc[:, half, :]).then_inc(sums_saved, 1)

            def take(b, base, stages, kind, i, j, number):
                frm = bank[number % 2]
                by_token = frm[:, :].rearrange("p (a c) -> p a c", a=4)
                blocks = slice(4 * i, 4 * i + 4)
                columns = slice(i * HALF, (i + 1) * HALF)

                def taken(instruction):
                    instruction.then_inc(job_taken, 1)

                def taken_by_self():
                    dve.wait_ge(job_taken, base + number + 1)

                dve.wait_ge(job_ready, base + number + 1)
                if kind == "mean":
                    taken(nc.vector.tensor_copy(group_stats[:, 0:1], frm[:, 0:1]))
                    taken_by_self()
                    link(nc.vector.tensor_tensor(group_stats[:, 1:2], channel_stats[:, 0:1], group_stats[:, 0:1],
                                                 ALU.subtract))
                    nc.vector.scalar_tensor_tensor(group_stats[:, 2:3], group_stats[:, 1:2], group_stats[:, 1:2],
                                                   channel_stats[:, 1:2], ALU.mult, ALU.add).then_inc(deviation_ready, 1)
                elif kind == "spread":
                    taken(nc.vector.tensor_copy(group_stats[:, 3:4], frm[:, 0:1]))
                    normalise_image(b)
                elif kind == "conv":
                    taken(nc.vector.scalar_tensor_tensor(layer0[:, columns], frm[:, :], bias_conv[:, 0:1],
                                                         image[:, columns], ALU.add, ALU.add))
                elif kind == "tokens":
                    if i == 0:
                        wait(dve, moved_on, b + 1)
                    taken(nc.vector.tensor_copy(tokens_new[:, blocks, :], by_token))
                    if i == 1:
                        taken_by_self()
                        layer_norm(b, int("finish" in stages), tokens_new, normed_new).then_inc(normed_ready, 1)
                        dve.wait_ge(normed_ready, b + 2)
                        link(nc.vector.tensor_tensor(angle[:], normed_new[:], everywhere(shift), ALU.add))
                        reduce_angle(angle[:], turns[:]).then_inc(angle_ready, 1)
                elif kind == "key":
                    taken(nc.vector.tensor_copy((queries if j else keys)[:, i, :], frm[:, :].bitcast(F16)))
                    if j == 1:
                        nc.vector.tensor_copy(values[:, :, 4 * i:4 * i + 4, 0:D],
                                              product[:].rearrange("p (a h) d -> p a h d", a=BLOCKS)
                                              [:, :, 4 * i:4 * i + 4, :]).then_inc(head_ready, 1)
                elif kind == "context":
                    by_head = frm[:, :].rearrange("p (h s) -> p h s", s=STRIP)
                    link(nc.vector.reciprocal(weight_inv[:, i % 2, :], by_head[:, :, D]))
                    taken(nc.vector.tensor_tensor(context[:, i, :].rearrange("p (h d) -> p h d", d=D),
                                                  by_head[:, :, 0:D],
                                                  weight_inv[:, i % 2, :].unsqueeze(2).broadcast_to([128, HEADS, D]),
                                                  ALU.mult))
                elif kind == "turn_context":
                    taken(nc.vector.tensor_copy(context_t[:, columns], frm[:, :]))
                elif kind == "combine":
                    taken(nc.vector.tensor_tensor(attended[:, blocks, :], by_token, normed_old[:, blocks, :], ALU.add))
                    if i == 1:
                        taken_by_self()
                        layer_norm(b, 0, attended, normed1).then_inc(normed1_ready, 1)
                elif kind == "features":
                    taken(nc.vector.tensor_copy(feature_t[:, columns], frm[0:FEATURES, :]))
                elif kind == "hidden":
                    taken(nc.vector.tensor_scalar(hidden[:, j, columns], frm[:, :], bias_hidden[:, j:j + 1], 0.0,
                                                  ALU.add, ALU.max))
                elif kind == "project":
                    if i == 0:
                        dve.wait_ge(x1_bias_ready, finishes(b) + 1)
                    taken(nc.vector.tensor_tensor(projected[:, blocks, :], by_token, x1_bias[:, blocks, :], ALU.add))
                    if i == 1:
                        taken_by_self()
                        layer_norm(b, 1 + int("prepare" in stages), projected, normed2).then_inc(normed2_ready, 1)
                elif kind == "turn_tokens":
                    taken(nc.vector.tensor_copy(normed3_t[:, columns], frm[:, :]))
                elif kind == "route":
                    taken(nc.vector.tensor_tensor(
                        logits[:, blocks, :], frm[:, 0:4 * EXPERTS].rearrange("p (a e) -> p a e", a=4),
                        bias_router[:].unsqueeze(1).broadcast_to([128, 4, EXPERTS]), ALU.add))
                    if i == 1:
                        taken_by_self()
                        pick_experts(b)
                elif kind == "turn_gates":
                    taken(nc.vector.tensor_copy(gates_t[:, columns], frm[0:EXPERTS, :]))
                elif kind == "expert_bias":
                    taken(nc.vector.tensor_tensor(mixed[:, blocks, :], by_token, x2[:, blocks, :], ALU.add))
                    if i == 1:
                        taken_by_self()
                elif kind == "expert":
                    for n in range(4):
                        expert = 4 * j + n
                        last = nc.vector.scalar_tensor_tensor(mixed[:, i, :], frm[:, 128 * n:128 * (n + 1)],
                                                              gates[:, i, expert:expert + 1], mixed[:, i, :],
                                                              ALU.mult, ALU.add)
                        if n < 3:
                            link(last)
                    taken(last)
                    taken_by_self()
                elif kind == "image":
                    if i == 0:
                        wait(dve, image_stored, 16 * finishes(b))
                    taken(nc.vector.tensor_copy(image_out[:, columns], frm[:, :]))

            def step(b):
                stages = stages_of(b)
                jobs, base, where = job_counter(b)
                done[0] = 0
                for group in range(GROUPS):
                    if group % 8 == 0 and group and "attend" in stages:
                        save_sums(b, group // 8 - 1)
                    if group == 2 and "prepare" in stages:
                        channel_moments(b)
                    if group == 24 and "finish" in stages:
                        dve.wait_ge(x1_ready, finishes(b) + 1)
                        link(nc.vector.tensor_scalar(feature_angle[:], x1[:, :, 0:FEATURES], math.pi / 2.0, None, ALU.add))
                        reduce_angle(feature_angle[:], feature_turns[:]).then_inc(feature_angle_ready, 1)
                    if group == 32 and "finish" in stages:
                        dve.wait_ge(feature_cos_ready, finishes(b) + 1)
                        nc.vector.tensor_tensor(feature[:], feature_cos[:], everywhere(cos_ry),
                                                ALU.mult).then_inc(feature_ready, 1)
                    if group == 33 and "prepare" in stages:
                        cosine_products(b)
                    if group == 46 and "finish" in stages:
                        dve.wait_ge(x2_ready, finishes(b) + 1)
                        layer_norm(b, 2 + int("prepare" in stages), x2, normed3).then_inc(normed3_ready, 1)
                    for at, kind, i, j, number in jobs:
                        if at == group and (kind != "conv" or j == LAST_TAPS):
                            take(b, base, stages, kind, i, j, number)
                if "attend" in stages:
                    save_sums(b, 2 * QUADS - 1)
                dve.sem_clear(vector_step)

            steps(dve, step)


def kernel(x, L0_conv_weight, L0_conv_bias, L1_attn_rx_theta, L1_attn_ry_theta, L1_attn_w_comb, L1_attn_b_comb,
           L1_attn_w1, L1_attn_b1, L1_attn_w2, L1_attn_b2, L1_attn_g1, L1_attn_beta1, L1_attn_g2, L1_attn_beta2,
           L1_ffn_router_w, L1_ffn_router_b, L1_ffn_expert_w, L1_ffn_expert_b):
    import concourse.bacc as bacc
    from concourse.bass_utils import run_bass_kernel_spmd

    def rows(row, times=1):
        return np.tile(np.asarray(row)[None, :], (128, times))

    laid_out = {
        "x": np.asarray(x).reshape(IMAGES, C, TOKENS),
        "conv_w": np.asarray(L0_conv_weight).transpose(1, 2, 3, 0).reshape(C, 9, C),
        "conv_b": np.asarray(L0_conv_bias).reshape(C, 1),
        "group_mean": np.kron(np.eye(C // GROUP_CHANNELS), np.ones((GROUP_CHANNELS, GROUP_CHANNELS))).astype(np.float32)
        / np.float32(GROUP_CHANNELS),
        "identity": np.eye(128, dtype=np.float32),
        "theta": rows(L1_attn_rx_theta, HEADS),
        "ry": rows(L1_attn_ry_theta),
        "w_comb": np.asarray(L1_attn_w_comb).T,
        "b_comb": rows(L1_attn_b_comb),
        "w1": np.asarray(L1_attn_w1).T,
        "b1": np.asarray(L1_attn_b1).reshape(CHUNKS, 128).T,
        "w2": np.asarray(L1_attn_w2).reshape(C, CHUNKS, 128).transpose(2, 1, 0),
        "b2": rows(L1_attn_b2),
        "g1": rows(L1_attn_g1),
        "beta1": rows(L1_attn_beta1),
        "g2": rows(L1_attn_g2),
        "beta2": rows(L1_attn_beta2),
        "router_w": np.asarray(L1_ffn_router_w),
        "router_b": rows(L1_ffn_router_b),
        "expert_w": np.asarray(L1_ffn_expert_w).transpose(1, 0, 2).reshape(C, EXPERTS * C),
        "expert_b": np.asarray(L1_ffn_expert_b),
        "earlier": np.tile(np.tril(np.ones((EXPERTS, EXPERTS), np.float32), -1)[None], (128, 1, 1)),
    }
    nc = bacc.Bacc("TRN2", target_bir_lowering=False, num_devices=1)
    arrays, args = {}, []
    for name, array in laid_out.items():
        array = np.ascontiguousarray(array)
        arrays[f"in_{name}"] = array
        args.append(nc.dram_tensor(f"in_{name}", array.shape, mybir.dt.from_np(array.dtype), kind="ExternalInput").ap())
    out = nc.dram_tensor("out_image", (IMAGES, C, TOKENS), F32, kind="ExternalOutput").ap()
    conv_hybrid(nc, *args, out)
    result = run_bass_kernel_spmd(nc, [arrays], core_ids=[0])
    return result.results[0]["out_image"].reshape(IMAGES, C, SIDE, SIDE)
```

```python
import math
from contextlib import ExitStack

import numpy as np
import concourse.bass as bass
from concourse import mybir

F32 = mybir.dt.float32
F16 = mybir.dt.float16
BF16 = mybir.dt.bfloat16
ALU = mybir.AluOpType
ACT = mybir.ActivationFunctionType
AX = mybir.AxisListType

IMAGES, C, SIDE, TOKENS = 32, 128, 32, 1024
PADDED = SIDE + 2
GROUP_CHANNELS = 4
BLOCKS = TOKENS // 128
HALF = TOKENS // 2
HEADS, D = 16, 8
QUADS = HEADS // 4
FEATURES, HIDDEN, CHUNKS = 8, 512, 4
PARTS = 3
STACK = PARTS * PARTS * FEATURES
EXPERTS, CHOSEN = 8, 2
GROUPS = QUADS * 2 * BLOCKS
PAIRS = 2 * GROUPS
RING = 4
STRIP = 32
SPLIT = 1024.0
SCORE_SCALE = 1.0 / (math.sqrt(D) * SPLIT * SPLIT)
ROUND = 1.5 * 2.0 ** 23
TURN_HI = 6.28125
TURN_LO = 2.0 * math.pi - 6.28125
HALF_SINE = (0.7071067781556869, -0.029462767169504807, 0.00036827228376790403,
             -2.1886103953064436e-06, 7.195782692868076e-09)
EPS = 1e-5


def schedule():
    jobs = [(3, "attend", "key", 3, v) for v in range(2)]
    jobs += [(1 + i, "finish", "context", i, 0) for i in range(BLOCKS)]
    jobs += [(4, "prepare", "mean", 0, 0), (6, "prepare", "spread", 0, 0)]
    jobs += [(9, "finish", "turn_context", i, 0) for i in range(2)]
    jobs += [(10, "finish", "combine", i, 0) for i in range(2)]
    jobs += [(11 + i, "prepare", "conv", 0, i) for i in range(3)]
    jobs += [(17, "finish", "features", 0, 0)]
    jobs += [(18 + 2 * i + j // 2, "finish", "hidden", i, j) for i in range(2) for j in range(CHUNKS)]
    jobs += [(22 + i, "finish", "project", i, 0) for i in range(2)]
    jobs += [(25 + i, "prepare", "conv", 1, i) for i in range(3)]
    jobs += [(31, "finish", "turn_tokens", i, 0) for i in range(2)]
    jobs += [(32, "finish", "route", 0, 0), (32, "prepare", "tokens", 0, 0)]
    jobs += [(33, "finish", "route", 1, 0), (33, "prepare", "tokens", 1, 0)]
    jobs += [(38, "finish", "turn_gates", 0, 0)]
    jobs += [(39 + i, "finish", "expert_bias", i, 0) for i in range(2)]
    expert_groups = [*range(41, 49), 50, *range(52, 59)]
    jobs += [(expert_groups[2 * i + j], "finish", "expert", i, j) for i in range(BLOCKS) for j in range(2)]
    jobs += [(54 + 2 * h + v, "prepare", "key", h, v) for h in range(3) for v in range(2)]
    jobs += [(61 + i, "finish", "image", i, 0) for i in range(2)]
    return sorted(jobs, key=lambda job: job[0])


JOBS = schedule()
LAST_TAPS = 2


def numbered(stages):
    out, number = [], 0
    for group, stage, kind, i, j in JOBS:
        if stage in stages:
            out.append((group, kind, i, j, number))
            number += not (kind == "conv" and j < LAST_TAPS)
    return out, number


STEADY = ("attend", "prepare", "finish")


def stages_of(b):
    if not isinstance(b, int):
        return STEADY
    return (("attend",) if 0 <= b < IMAGES else ()) + (("prepare",) if b + 1 < IMAGES else ()) \
        + (("finish",) if b >= 1 else ())


def before(b, count):
    if isinstance(b, int):
        return sum(count(stages_of(s)) for s in range(-1, b))
    first = count(stages_of(-1)) + count(stages_of(0))
    return (b - 1) * count(STEADY) + first


def conv_hybrid(nc, x, conv_w, conv_b, group_mean, identity, theta, ry, w_comb, b_comb, w1, b1, w2, b2,
                g1, beta1, g2, beta2, router_w, router_b, expert_w, expert_b, earlier, out):
    ctx = ExitStack()
    with ctx:
        def sb(name, shape, dtype=F32):
            return ctx.enter_context(nc.sbuf_tensor(name, shape, dtype))

        def sem(name):
            return ctx.enter_context(nc.semaphore(name))

        w_conv = sb("w_conv", [C, 9, C])
        bias_conv = sb("bias_conv", [C, 1])
        mean_of_group = sb("mean_of_group", [C, C])
        ident = sb("ident", [128, 128])
        ident16 = sb("ident16", [128, 128], F16)
        ident_bf16 = sb("ident_bf16", [128, 128], BF16)
        shift = sb("shift", [128, C])
        ry_angle = sb("ry_angle", [128, 3, FEATURES])
        w_combine = sb("w_combine", [C, C])
        bias_combine = sb("bias_combine", [128, C])
        w_hidden = sb("w_hidden", [STACK, HIDDEN], BF16)
        bias_hidden = sb("bias_hidden", [128, CHUNKS])
        w_project = sb("w_project", [128, CHUNKS, C])
        bias_project = sb("bias_project", [128, C])
        gain1 = sb("gain1", [128, C])
        offset1 = sb("offset1", [128, C])
        gain2 = sb("gain2", [128, C])
        offset2 = sb("offset2", [128, C])
        w_router = sb("w_router", [C, EXPERTS])
        bias_router = sb("bias_router", [128, EXPERTS])
        w_expert = sb("w_expert", [C, EXPERTS * C])
        bias_expert = sb("bias_expert", [BLOCKS * EXPERTS, BLOCKS, C])
        is_earlier = sb("is_earlier", [128, EXPERTS, EXPERTS])
        minus_half = sb("minus_half", [128, BLOCKS])
        eps = sb("eps", [128, BLOCKS])

        image = sb("image", [C, TOKENS])
        pixel_stats = sb("pixel_stats", [C, 2, 6])
        channel_stats = sb("channel_stats", [C, 2])
        group_stats = sb("group_stats", [C, 4])
        group_rstd = sb("group_rstd", [C, 2])
        padded = sb("padded", [C, PADDED, PADDED])
        layer0 = sb("layer0", [C, TOKENS])
        tokens_new = sb("tokens_new", [128, BLOCKS, C])
        normed_new = sb("normed_new", [128, BLOCKS, C])
        scratch = sb("scratch", [128, CHUNKS, TOKENS])
        angle, turns = (scratch[:, n, :].rearrange("p (a c) -> p a c", a=BLOCKS) for n in range(2))
        cosine = scratch[:, 2, :].rearrange("p (a c) -> p a c", a=BLOCKS)
        product = sb("product", [128, BLOCKS * HEADS, D])
        key_halves = sb("key_halves", [128, BLOCKS, HEADS, 4 * D], F16)
        query_halves = sb("query_halves", [128, BLOCKS, HEADS, 4 * D], F16)

        keys = sb("keys", [128, QUADS, TOKENS], F16)
        queries = sb("queries", [128, QUADS, TOKENS], F16)
        values = sb("values", [128, BLOCKS, HEADS, STRIP])
        probs = sb("probs", [128, RING, 2 * HALF])
        sums = sb("sums", [128, QUADS, TOKENS])

        tokens_mid = sb("tokens_mid", [128, BLOCKS, C])
        tokens_old = sb("tokens_old", [128, BLOCKS, C])
        normed_old = sb("normed_old", [128, BLOCKS, C])
        weight_inv = sb("weight_inv", [128, 2, HEADS])
        context = sb("context", [128, BLOCKS, C])
        context_t = sb("context_t", [C, TOKENS])
        attended = sb("attended", [128, BLOCKS, C])
        normed1 = sb("normed1", [128, BLOCKS, C])
        x1 = sb("x1", [128, BLOCKS, C])
        x1_bias = sb("x1_bias", [128, BLOCKS, C])
        feature_angle = sb("feature_angle", [128, BLOCKS, FEATURES])
        feature_turns = sb("feature_turns", [128, BLOCKS, FEATURES])
        feature_cos = sb("feature_cos", [128, BLOCKS, FEATURES])
        feature = sb("feature", [128, BLOCKS, FEATURES])
        feature_part = sb("feature_part", [128, PARTS, BLOCKS, FEATURES], BF16)
        feature_stack = sb("feature_stack", [128, BLOCKS, PARTS, PARTS, FEATURES], BF16)
        feature_t = sb("feature_t", [STACK, TOKENS], BF16)
        hidden = scratch
        w_hidden_rest = scratch[0:FEATURES, 0, :].rearrange("p (a f) -> p a f", a=2)
        w_hidden_part = scratch[0:FEATURES, 1:3, :].rearrange("p a f -> p (a f)").bitcast(BF16) \
            [:, 0:PARTS * HIDDEN].rearrange("p (a f) -> p a f", a=PARTS)
        projected = attended
        normed2 = sb("normed2", [128, BLOCKS, C])
        x2 = sb("x2", [128, BLOCKS, C])
        normed3, normed3_t = context, context_t
        logits = sb("logits", [128, BLOCKS, EXPERTS])
        top = sb("top", [128, BLOCKS])
        below = sb("below", [128, BLOCKS, EXPERTS])
        ahead_of = sb("ahead_of", [128, BLOCKS, EXPERTS, EXPERTS])
        tied = sb("tied", [128, BLOCKS, EXPERTS, EXPERTS])
        rank = sb("rank", [128, BLOCKS, EXPERTS])
        weight = sb("weight", [128, BLOCKS, EXPERTS])
        chosen = sb("chosen", [128, BLOCKS, EXPERTS])
        chosen_sum = sb("chosen_sum", [128, BLOCKS])
        chosen_inv = sb("chosen_inv", [128, BLOCKS])
        gates_wide = sb("gates_wide", [128, 2, BLOCKS, EXPERTS])
        gates = gates_wide[:, 0, :, :]
        gates_t = sb("gates_t", [BLOCKS * EXPERTS, 128])
        mixed = x2
        image_out = sb("image_out", [C, TOKENS])
        block_stats = sb("block_stats", [128, BLOCKS, 6])
        token_stats = sb("token_stats", [128, BLOCKS, 2])
        variance = sb("variance", [128, BLOCKS])
        rstd = sb("rstd", [128, BLOCKS])

        scores = [ctx.enter_context(nc.psum_tensor(f"scores{n}", [128, 2 * HALF], F32)) for n in range(2)]
        sums_acc = ctx.enter_context(nc.psum_tensor("sums_acc", [128, 2, HALF], F32))
        bank = [ctx.enter_context(nc.psum_tensor(f"bank{n}", [128, HALF], F32)) for n in range(2)]

        weights_loaded = sem("weights_loaded")
        w_hidden_split, w_hidden_stacked = sem("w_hidden_split"), sem("w_hidden_stacked")
        image_loaded = sem("image_loaded")
        filled = sem("filled")
        job_ready = sem("job_ready")
        job_taken = sem("job_taken")
        scores_ready = sem("scores_ready")
        probs_ready = sem("probs_ready")
        probs_used = sem("probs_used")
        sums_saved = sem("sums_saved")
        head_ready = sem("head_ready")
        moments_ready = sem("moments_ready")
        deviation_ready = sem("deviation_ready")
        group_rstd_ready = sem("group_rstd_ready")
        padded_ready = sem("padded_ready")
        stats_ready = sem("stats_ready")
        rstd_ready = sem("rstd_ready")
        moved_on = sem("moved_on")
        normed_ready = sem("normed_ready")
        angle_ready = sem("angle_ready")
        halves_ready = sem("halves_ready")
        normed1_ready, x1_ready = sem("normed1_ready"), sem("x1_ready")
        normed2_ready, x2_ready = sem("normed2_ready"), sem("x2_ready")
        x1_bias_ready = sem("x1_bias_ready")
        feature_ready = sem("feature_ready")
        normed3_ready = sem("normed3_ready")
        below_ready, weight_ready = sem("below_ready"), sem("weight_ready")
        gates_ready = sem("gates_ready")
        image_stored = sem("image_stored")
        vector_step = sem("vector_step")
        pool_step = sem("pool_step")

        loads = [(w_conv, conv_w), (bias_conv, conv_b), (mean_of_group, group_mean), (ident, identity),
                 (shift, theta), (ry_angle[:, 0, :], ry), (w_combine, w_comb), (bias_combine, b_comb),
                 (w_hidden_rest[:, 0, :], w1), (bias_hidden, b1), (w_project, w2), (bias_project, b2), (gain1, g1),
                 (offset1, beta1), (gain2, g2), (offset2, beta2), (w_router, router_w),
                 (bias_router, router_b), (w_expert, expert_w), (bias_expert, expert_b),
                 (is_earlier, earlier)]
        FILLS = 8

        def everywhere(row):
            return row[:, :].unsqueeze(1).broadcast_to([128, BLOCKS, row.shape[1]])

        def finishes(b):
            return before(b, lambda stages: int("finish" in stages))

        def job_counter(b):
            jobs, _ = numbered(stages_of(b))
            base = before(b, lambda stages: numbered(stages)[1])
            where = {(kind, i, j): number for _, kind, i, j, number in jobs}
            return jobs, base, where

        def wait(engine, semaphore, value):
            if not isinstance(value, int) or value > 0:
                engine.wait_ge(semaphore, value)

        def steps(engine, body):
            body(-1)
            body(0)
            with engine.Fori(1, IMAGES - 1) as b:
                body(b)
            body(IMAGES - 1)
            body(IMAGES)

        block = ctx.enter_context(nc.Block())

        @block.sync
        def _(sp):
            for tile, source in loads:
                sp.dma_start(tile if isinstance(tile, bass.AP) else tile[:], source).then_inc(weights_loaded, 16)
            sp.wait_ge(w_hidden_split, 1)
            for pairing in range(PARTS * PARTS):
                sp.dma_start(w_hidden[FEATURES * pairing:FEATURES * (pairing + 1), :],
                             w_hidden_part[:, pairing % PARTS, :]).then_inc(w_hidden_stacked, 16)

            def step(b):
                stages = stages_of(b)
                jobs, base, where = job_counter(b)
                if "prepare" in stages:
                    wait(sp, normed_ready, b + 1)
                    sp.dma_start(image[:], x[b + 1, :, :]).then_inc(image_loaded, 16)
                if "finish" in stages:
                    wait(sp, job_taken, base + where["image", 1, 0] + 1)
                    sp.dma_start(out[b - 1, :, :], image_out[:]).then_inc(image_stored, 16)

            steps(sp, step)
            sp.wait_ge(image_stored, 16 * IMAGES)

        @block.tensor
        def _(pe):
            pe.wait_ge(weights_loaded, 16 * len(loads))
            pe.wait_ge(filled, FILLS)
            pe.wait_ge(w_hidden_stacked, 16 * PARTS * PARTS)

            def score_pair(b, group, pair):
                quad, half, blk = group // 16, group // 8 % 2, group % 8
                wait(pe, probs_ready, b * PAIRS + 2 * group + pair - 1)
                for n in range(2):
                    head = 2 * pair + n
                    rows = slice(STRIP * head, STRIP * (head + 1))
                    last = nc.tensor.matmul(scores[pair][:, n * HALF:(n + 1) * HALF],
                                            keys[rows, quad, 128 * blk:128 * (blk + 1)],
                                            queries[rows, quad, half * HALF:(half + 1) * HALF],
                                            start=True, stop=True)
                last.then_inc(scores_ready, 1)

            def first_scores(b):
                pe.wait_ge(head_ready, b * QUADS + 1)
                score_pair(b, 0, 0)
                score_pair(b, 0, 1)

            def sum_group(b, group):
                quad, half, blk = group // 16, group // 8 % 2, group % 8
                unit = 2 * quad + half
                if blk == 0:
                    wait(pe, sums_saved, b * 2 * QUADS + unit - 1)
                pe.wait_ge(probs_ready, b * PAIRS + 2 * group + 2)
                for head in range(4):
                    pair = 2 * group + head // 2
                    last = nc.tensor.matmul(sums_acc[STRIP * head:STRIP * (head + 1), half, :],
                                            values[:, blk, 4 * quad + head, :],
                                            probs[:, pair % RING, (head % 2) * HALF:(head % 2 + 1) * HALF],
                                            start=(blk == 0), stop=(blk == BLOCKS - 1))
                last.then_inc(probs_used, 1)

            def job(b, base, where, kind, i, j, number):
                to = bank[number % 2]

                def taken(*which):
                    pe.wait_ge(job_taken, base + where[which] + 1)

                if kind != "conv" or j == 0:
                    wait(pe, job_taken, base + number - 1)
                if kind == "mean":
                    pe.wait_ge(moments_ready, b + 2)
                    last = nc.tensor.matmul(to[:, 0:1], mean_of_group[:], channel_stats[:, 0:1], start=True, stop=True)
                elif kind == "spread":
                    pe.wait_ge(deviation_ready, b + 2)
                    last = nc.tensor.matmul(to[:, 0:1], mean_of_group[:], group_stats[:, 2:3], start=True, stop=True)
                elif kind == "conv":
                    if j == 0:
                        pe.wait_ge(padded_ready, b + 2)
                    for tap in range(3 * j, 3 * j + 3):
                        row = i * SIDE // 2 + tap // 3
                        last = nc.tensor.matmul(to[:, :], w_conv[:, tap, :],
                                                padded[:, row:row + SIDE // 2, tap % 3:tap % 3 + SIDE],
                                                start=(tap == 0), stop=(tap == 8))
                elif kind in ("tokens", "turn_context", "turn_tokens", "image"):
                    if kind == "tokens":
                        taken("conv", i, LAST_TAPS)
                    elif kind == "turn_context":
                        taken("context", 4 * i + 3, 0)
                    elif kind == "turn_tokens":
                        pe.wait_ge(normed3_ready, finishes(b) + 1)
                    else:
                        taken("expert", 4 * i + 3, 1)
                    source = {"turn_context": context, "turn_tokens": normed3, "image": mixed}
                    for n in range(4):
                        blk = 4 * i + n
                        piece = layer0[:, 128 * blk:128 * (blk + 1)] if kind == "tokens" else source[kind][:, blk, :]
                        last = nc.tensor.transpose(to[:, 128 * n:128 * (n + 1)], piece, ident[:])
                elif kind == "key":
                    of_next = 0 if i == QUADS - 1 else 1
                    pe.wait_ge(halves_ready, b + 1 + of_next)
                    for blk in range(BLOCKS):
                        piece = (query_halves if j else key_halves)[:, blk, 4 * i:4 * i + 4, :]
                        last = nc.tensor.transpose(to[:, :].bitcast(F16)[:, 128 * blk:128 * (blk + 1)],
                                                   piece.rearrange("p h d -> p (h d)"), ident16[:])
                elif kind == "context":
                    if i == 0:
                        pe.wait_ge(sums_saved, b * 2 * QUADS)
                    for quad in range(QUADS):
                        last = nc.tensor.transpose(to[:, 128 * quad:128 * (quad + 1)],
                                                   sums[:, quad, 128 * i:128 * (i + 1)], ident[:])
                elif kind == "combine":
                    taken("turn_context", i, 0)
                    for n in range(4):
                        last = nc.tensor.matmul(to[:, 128 * n:128 * (n + 1)],
                                                context_t[:, 128 * (4 * i + n):128 * (4 * i + n + 1)],
                                                w_combine[:], start=True, stop=True)
                elif kind == "features":
                    pe.wait_ge(feature_ready, finishes(b) + 1)
                    for blk in range(BLOCKS):
                        last = nc.tensor.transpose(to[0:STACK, :].bitcast(BF16)[:, 128 * blk:128 * (blk + 1)],
                                                   feature_stack[:, blk, :, :, :].rearrange("p a b f -> p (a b f)"),
                                                   ident_bf16[:])
                elif kind == "turn_gates":
                    pe.wait_ge(gates_ready, finishes(b) + 1)
                    last = nc.tensor.transpose(to[:, 0:128], gates_wide[:].rearrange("p z a e -> p (z a e)"), ident[:])
                elif kind == "hidden":
                    taken("features", 0, 0)
                    last = nc.tensor.matmul(to[:, :], w_hidden[:, 128 * j:128 * (j + 1)],
                                            feature_t[:, i * HALF:(i + 1) * HALF], start=True, stop=True)
                elif kind == "project":
                    taken("hidden", i, CHUNKS - 1)
                    for n in range(4):
                        at = 128 * (4 * i + n)
                        for chunk in range(CHUNKS):
                            last = nc.tensor.matmul(to[:, 128 * n:128 * (n + 1)], hidden[:, chunk, at:at + 128],
                                                    w_project[:, chunk, :],
                                                    start=(chunk == 0), stop=(chunk == CHUNKS - 1))
                elif kind == "route":
                    taken("turn_tokens", i, 0)
                    for n in range(4):
                        last = nc.tensor.matmul(to[:, EXPERTS * n:EXPERTS * (n + 1)],
                                                normed3_t[:, 128 * (4 * i + n):128 * (4 * i + n + 1)],
                                                w_router[:], start=True, stop=True)
                elif kind == "expert_bias":
                    taken("turn_gates", 0, 0)
                    last = nc.tensor.matmul(to[:, :], gates_t[:],
                                            bias_expert[:, 4 * i:4 * i + 4, :].rearrange("p a c -> p (a c)"),
                                            start=True, stop=True)
                elif kind == "expert":
                    last = nc.tensor.matmul(to[:, :], normed3_t[:, 128 * i:128 * (i + 1)],
                                            w_expert[:, j * HALF:(j + 1) * HALF], start=True, stop=True)
                if kind != "conv" or j == LAST_TAPS:
                    last.then_inc(job_ready, 1)

            def step(b):
                stages = stages_of(b)
                jobs, base, where = job_counter(b)
                for group in range(GROUPS):
                    if "attend" in stages:
                        if group + 1 < GROUPS:
                            if (group + 1) % 16 == 0:
                                pe.wait_ge(head_ready, b * QUADS + (group + 1) // 16 + 1)
                            score_pair(b, group + 1, 0)
                            score_pair(b, group + 1, 1)
                        elif "prepare" in stages:
                            first_scores(b + 1)
                        sum_group(b, group)
                    for at, kind, i, j, number in jobs:
                        if at == group:
                            job(b, base, where, kind, i, j, number)
                if "attend" not in stages and "prepare" in stages:
                    first_scores(b + 1)

            steps(pe, step)

        @block.scalar
        def _(act):
            def gate_exponentials(b):
                act.wait_ge(below_ready, finishes(b) + 1)
                nc.scalar.activation(weight[:], below[:], ACT.Exp).then_inc(weight_ready, 1)

            def step(b):
                stages = stages_of(b)
                for pair in range(PAIRS):
                    if "attend" in stages:
                        act.wait_ge(scores_ready, b * PAIRS + pair + 1)
                        if pair % 2 == 0:
                            wait(act, probs_used, b * GROUPS + pair // 2 - RING // 2 + 1)
                        nc.scalar.activation(probs[:, pair % RING, :], scores[pair % 2][:, :], ACT.Exp,
                                             scale=SCORE_SCALE).then_inc(probs_ready, 1)
                    if pair == 2 * 35 + 1 and "finish" in stages:
                        gate_exponentials(b)

            steps(act, step)

        @block.gpsimd
        def _(pool):
            nc.gpsimd.memset(minus_half[:], -0.5).then_inc(filled, 1)
            nc.gpsimd.memset(eps[:], EPS).then_inc(filled, 1)
            nc.gpsimd.memset(padded[:], 0.0).then_inc(filled, 1)
            pool.wait_ge(filled, FILLS)
            pool.wait_ge(weights_loaded, 16 * len(loads))
            done = [0]

            def link(instruction):
                instruction.then_inc(pool_step, 1)
                done[0] += 1
                pool.wait_ge(pool_step, done[0])

            def layer_rstd(b, n):
                base = before(b, lambda stages: ("prepare" in stages) + 3 * ("finish" in stages))
                pool.wait_ge(stats_ready, base + n + 1)
                link(nc.gpsimd.tensor_tensor(variance[:], token_stats[:, :, 1], eps[:], ALU.add))
                nc.gpsimd.tensor_tensor(rstd[:], variance[:], minus_half[:], ALU.pow).then_inc(rstd_ready, 1)

            def step(b):
                stages = stages_of(b)
                jobs, base, where = job_counter(b)
                done[0] = 0
                n = 0
                if "prepare" in stages:
                    pool.wait_ge(job_taken, base + where["spread", 0, 0] + 1)
                    link(nc.gpsimd.tensor_tensor(group_rstd[:, 0:1], group_stats[:, 3:4], eps[:, 0:1], ALU.add))
                    nc.gpsimd.tensor_tensor(group_rstd[:, 1:2], group_rstd[:, 0:1], minus_half[:, 0:1],
                                            ALU.pow).then_inc(group_rstd_ready, 1)
                if "finish" in stages:
                    layer_rstd(b, n)
                    n += 1
                    pool.wait_ge(normed1_ready, finishes(b) + 1)
                    link(nc.gpsimd.tensor_tensor(normed1[:], normed1[:], everywhere(gain1), ALU.mult))
                    nc.gpsimd.tensor_tensor(x1[:], normed1[:], everywhere(offset1), ALU.add).then_inc(x1_ready, 1)
                    pool.wait_ge(x1_ready, finishes(b) + 1)
                    nc.gpsimd.tensor_tensor(x1_bias[:], x1[:], everywhere(bias_project),
                                            ALU.add).then_inc(x1_bias_ready, 1)
                    nc.gpsimd.tensor_tensor(tokens_old[:], tokens_mid[:], everywhere(offset2), ALU.add)
                if "attend" in stages:
                    wait(pool, normed_ready, b + 1)
                    nc.gpsimd.tensor_tensor(normed_old[:], normed_new[:], everywhere(bias_combine),
                                            ALU.add).then_inc(moved_on, 1)
                if "finish" in stages:
                    layer_rstd(b, n)
                    n += 1
                if "finish" in stages:
                    pool.wait_ge(normed2_ready, finishes(b) + 1)
                    link(nc.gpsimd.tensor_tensor(normed2[:], normed2[:], everywhere(gain2), ALU.mult))
                    nc.gpsimd.tensor_tensor(x2[:], normed2[:], tokens_old[:], ALU.add).then_inc(x2_ready, 1)
                    layer_rstd(b, n)
                    n += 1
                if "prepare" in stages:
                    layer_rstd(b, n)
                    pool.wait_ge(normed_ready, b + 2)
                    nc.gpsimd.tensor_tensor(angle, normed_new[:], everywhere(shift), ALU.add).then_inc(angle_ready, 1)
                pool.sem_clear(pool_step)

            steps(pool, step)

        @block.vector
        def _(dve):
            done = [0]

            def link(instruction):
                instruction.then_inc(vector_step, 1)
                done[0] += 1
                dve.wait_ge(vector_step, done[0])

            def reduce_angle(w, turn):
                link(nc.vector.tensor_scalar(turn, w, 1.0 / (2.0 * math.pi), ROUND, ALU.mult, ALU.add))
                link(nc.vector.tensor_scalar(turn, turn, ROUND, None, ALU.subtract))
                link(nc.vector.scalar_tensor_tensor(w, turn, -TURN_HI, w, ALU.mult, ALU.add))
                return nc.vector.scalar_tensor_tensor(w, turn, -TURN_LO, w, ALU.mult, ALU.add)

            def half_sine(w, square, to):
                link(nc.vector.tensor_tensor(square, w, w, ALU.mult))
                link(nc.vector.tensor_scalar(to, square, HALF_SINE[-1], None, ALU.mult))
                for coefficient in HALF_SINE[-2:0:-1]:
                    link(nc.vector.scalar_tensor_tensor(to, to, coefficient, square, ALU.add, ALU.mult))

            def from_half_sine(w, square, to):
                link(nc.vector.scalar_tensor_tensor(w, to, HALF_SINE[0], w, ALU.add, ALU.mult))
                link(nc.vector.tensor_tensor(square, w, w, ALU.mult))
                return nc.vector.tensor_scalar(to, square, -1.0, 1.0, ALU.mult, ALU.add)

            def split(whole, parts, rest):
                link(nc.vector.tensor_copy(parts[0], whole))
                link(nc.vector.tensor_tensor(rest, whole, parts[0], ALU.subtract))
                link(nc.vector.tensor_copy(parts[1], rest))
                link(nc.vector.tensor_tensor(rest, rest, parts[1], ALU.subtract))
                return nc.vector.tensor_copy(parts[2], rest)

            nc.vector.memset(gates_wide[:, 1, :, :], 0.0).then_inc(filled, 1)
            nc.vector.memset(values[:, :, :, D + 1:STRIP], 0.0).then_inc(filled, 1)
            nc.vector.memset(values[:, :, :, D:D + 1], 1.0).then_inc(filled, 1)
            dve.wait_ge(weights_loaded, 16 * len(loads))
            nc.vector.tensor_copy(ident16[:], ident[:]).then_inc(filled, 1)
            nc.vector.tensor_copy(ident_bf16[:], ident[:]).then_inc(filled, 1)
            split(w_hidden_rest[:, 0, :], [w_hidden_part[:, n, :] for n in range(PARTS)],
                  w_hidden_rest[:, 1, :]).then_inc(w_hidden_split, 1)
            link(reduce_angle(ry_angle[:, 0, :], ry_angle[:, 1, :]))
            half_sine(ry_angle[:, 0, :], ry_angle[:, 1, :], ry_angle[:, 2, :])
            link(from_half_sine(ry_angle[:, 0, :], ry_angle[:, 1, :], ry_angle[:, 2, :]))
            cos_ry = ry_angle[:, 2, :]
            dve.wait_ge(filled, FILLS)
            dve.wait_ge(w_hidden_stacked, 16 * PARTS * PARTS)
            dve.sem_clear(vector_step)

            def channel_moments(b):
                dve.wait_ge(image_loaded, 16 * (b + 2))
                nc.vector.bn_stats(pixel_stats[:, 0, :], image[:, 0:HALF])
                link(nc.vector.bn_stats(pixel_stats[:, 1, :], image[:, HALF:TOKENS]))
                nc.vector.bn_aggr(channel_stats[:], pixel_stats[:].rearrange("p a s -> p (a s)")).then_inc(moments_ready, 1)

            def normalise_image(b):
                dve.wait_ge(group_rstd_ready, b + 2)
                nc.vector.tensor_scalar(padded[:, 1:SIDE + 1, 1:SIDE + 1],
                                        image[:].rearrange("p (r c) -> p r c", c=SIDE),
                                        group_stats[:, 0:1], group_rstd[:, 1:2],
                                        ALU.subtract, ALU.mult).then_inc(padded_ready, 1)

            def token_moments(source):
                for blk in range(BLOCKS - 1):
                    nc.vector.bn_stats(block_stats[:, blk, :], source[:, blk, :])
                link(nc.vector.bn_stats(block_stats[:, BLOCKS - 1, :], source[:, BLOCKS - 1, :]))
                for blk in range(BLOCKS):
                    last = nc.vector.bn_aggr(token_stats[:, blk, :], block_stats[:, blk, :])
                last.then_inc(stats_ready, 1)

            def normalise(b, n, source, target):
                base = before(b, lambda stages: ("prepare" in stages) + 3 * ("finish" in stages))
                dve.wait_ge(rstd_ready, base + n + 1)
                for blk in range(BLOCKS):
                    last = nc.vector.tensor_scalar(target[:, blk, :], source[:, blk, :], token_stats[:, blk, 0:1],
                                                   rstd[:, blk:blk + 1], ALU.subtract, ALU.mult)
                return last

            def layer_norm(b, n, source, target):
                token_moments(source)
                return normalise(b, n, source, target)

            def stack_features():
                link(nc.vector.tensor_tensor(feature[:], feature_cos[:],
                                             cos_ry.unsqueeze(1).broadcast_to([128, BLOCKS, FEATURES]), ALU.mult))
                link(split(feature[:], [feature_part[:, n, :, :] for n in range(PARTS)], feature_turns[:]))
                for n in range(PARTS):
                    last = nc.vector.tensor_copy(
                        feature_stack[:, :, n, :, :],
                        feature_part[:, n, :, :].unsqueeze(2).broadcast_to([128, BLOCKS, PARTS, FEATURES]))
                last.then_inc(feature_ready, 1)

            COSINE_PARTS = 9

            def cosine_part(part):
                w, square, to = angle, turns, cosine
                if part == 0:
                    link(nc.vector.tensor_scalar(turns, w, 1.0 / (2.0 * math.pi), ROUND, ALU.mult, ALU.add))
                    link(nc.vector.tensor_scalar(turns, turns, ROUND, None, ALU.subtract))
                elif part == 1:
                    link(nc.vector.scalar_tensor_tensor(w, turns, -TURN_HI, w, ALU.mult, ALU.add))
                elif part == 2:
                    link(nc.vector.scalar_tensor_tensor(w, turns, -TURN_LO, w, ALU.mult, ALU.add))
                elif part == 3:
                    link(nc.vector.tensor_tensor(square, w, w, ALU.mult))
                    link(nc.vector.tensor_scalar(to, square, HALF_SINE[4], None, ALU.mult))
                elif part < 7:
                    link(nc.vector.scalar_tensor_tensor(to, to, HALF_SINE[7 - part], square, ALU.add, ALU.mult))
                elif part == 7:
                    link(nc.vector.scalar_tensor_tensor(w, to, HALF_SINE[0], w, ALU.add, ALU.mult))
                else:
                    link(nc.vector.tensor_tensor(square, w, w, ALU.mult))
                    link(nc.vector.tensor_scalar(to, square, -1.0, 1.0, ALU.mult, ALU.add))

            def cosine_products(part):
                by_head = scratch[:, 2, :].rearrange("p (h d) -> p h d", d=D)
                cos = [by_head[:, :, d] for d in range(D)]
                if part == 0:
                    nc.vector.tensor_tensor(product[:, :, 0], cos[1], cos[2], ALU.mult)
                    link(nc.vector.tensor_tensor(product[:, :, 1], cos[0], cos[1], ALU.mult))
                for d in range(2, 5) if part == 0 else range(5, D):
                    if d + 1 < D:
                        nc.vector.tensor_tensor(product[:, :, 0], product[:, :, 0], cos[d + 1], ALU.mult)
                    link(nc.vector.tensor_tensor(product[:, :, d], product[:, :, d - 1], cos[d], ALU.mult))

            def split_products(part):
                as_keys = key_halves[:].rearrange("p a h (r d) -> p (a h) r d", r=4)
                as_queries = query_halves[:].rearrange("p a h (r d) -> p (a h) r d", r=4)
                if part == 0:
                    link(nc.vector.tensor_scalar(as_keys[:, :, 0, :], product[:], SPLIT, None, ALU.mult))
                    link(nc.vector.scalar_tensor_tensor(as_keys[:, :, 1, :], product[:], SPLIT, as_keys[:, :, 0, :],
                                                        ALU.mult, ALU.subtract))
                elif part == 1:
                    nc.vector.tensor_copy(as_keys[:, :, 2:4, :], as_keys[:, :, 0:2, :])
                    nc.vector.tensor_copy(as_queries[:, :, 2, :], as_keys[:, :, 1, :])
                else:
                    nc.vector.tensor_copy(as_queries[:, :, 0:2, :], as_keys[:, :, 0:2, :])
                    nc.vector.tensor_copy(as_queries[:, :, 3, :], as_keys[:, :, 0, :]).then_inc(halves_ready, 1)

            gate_shape = [128, BLOCKS, EXPERTS]

            def rank_experts():
                all_pairs = [128, BLOCKS, EXPERTS, EXPERTS]
                link(nc.vector.tensor_reduce(top[:], logits[:], axis=AX.X, op=ALU.max))
                nc.vector.tensor_tensor(below[:], logits[:], top[:].unsqueeze(2).broadcast_to(gate_shape),
                                        ALU.subtract).then_inc(below_ready, 1)
                other, own = (logits[:].unsqueeze(2).broadcast_to(all_pairs),
                              logits[:].unsqueeze(3).broadcast_to(all_pairs))
                nc.vector.tensor_tensor(ahead_of[:], other, own, ALU.is_gt)
                link(nc.vector.tensor_tensor(tied[:], other, own, ALU.is_equal))
                link(nc.vector.tensor_tensor(tied[:], tied[:], is_earlier[:].unsqueeze(1).broadcast_to(all_pairs),
                                             ALU.mult))
                link(nc.vector.tensor_tensor(ahead_of[:], ahead_of[:], tied[:], ALU.add))
                link(nc.vector.tensor_reduce(rank[:], ahead_of[:], axis=AX.X, op=ALU.add))

            def weigh_experts(b):
                dve.wait_ge(weight_ready, finishes(b) + 1)
                link(nc.vector.scalar_tensor_tensor(chosen[:], rank[:], float(CHOSEN), weight[:], ALU.is_lt, ALU.mult))
                link(nc.vector.tensor_reduce(chosen_sum[:], chosen[:], axis=AX.X, op=ALU.add))
                link(nc.vector.reciprocal(chosen_inv[:], chosen_sum[:]))
                nc.vector.tensor_tensor(gates, chosen[:], chosen_inv[:].unsqueeze(2).broadcast_to(gate_shape),
                                        ALU.mult).then_inc(gates_ready, 1)

            def save_sums(b, unit):
                quad, half = unit // 2, unit % 2
                dve.wait_ge(probs_used, b * GROUPS + BLOCKS * (unit + 1))
                nc.vector.tensor_copy(sums[:, quad, half * HALF:(half + 1) * HALF],
                                      sums_acc[:, half, :]).then_inc(sums_saved, 1)

            def take(b, base, stages, kind, i, j, number):
                frm = bank[number % 2]
                by_token = frm[:, :].rearrange("p (a c) -> p a c", a=4)
                blocks = slice(4 * i, 4 * i + 4)
                columns = slice(i * HALF, (i + 1) * HALF)

                def taken(instruction):
                    instruction.then_inc(job_taken, 1)

                def taken_by_self():
                    dve.wait_ge(job_taken, base + number + 1)

                dve.wait_ge(job_ready, base + number + 1)
                if kind == "mean":
                    taken(nc.vector.tensor_copy(group_stats[:, 0:1], frm[:, 0:1]))
                    taken_by_self()
                    link(nc.vector.tensor_tensor(group_stats[:, 1:2], channel_stats[:, 0:1], group_stats[:, 0:1],
                                                 ALU.subtract))
                    nc.vector.scalar_tensor_tensor(group_stats[:, 2:3], group_stats[:, 1:2], group_stats[:, 1:2],
                                                   channel_stats[:, 1:2], ALU.mult, ALU.add).then_inc(deviation_ready, 1)
                elif kind == "spread":
                    taken(nc.vector.tensor_copy(group_stats[:, 3:4], frm[:, 0:1]))
                    normalise_image(b)
                elif kind == "conv":
                    taken(nc.vector.scalar_tensor_tensor(layer0[:, columns], frm[:, :], bias_conv[:, 0:1],
                                                         image[:, columns], ALU.add, ALU.add))
                elif kind == "tokens":
                    taken(nc.vector.tensor_copy(tokens_new[:, blocks, :], by_token))
                    if i == 1:
                        taken_by_self()
                elif kind == "key":
                    taken(nc.vector.tensor_copy((queries if j else keys)[:, i, :], frm[:, :].bitcast(F16)))
                    if j == 1:
                        nc.vector.tensor_copy(values[:, :, 4 * i:4 * i + 4, 0:D],
                                              product[:].rearrange("p (a h) d -> p a h d", a=BLOCKS)
                                              [:, :, 4 * i:4 * i + 4, :]).then_inc(head_ready, 1)
                elif kind == "context":
                    by_head = frm[:, :].rearrange("p (h s) -> p h s", s=STRIP)
                    link(nc.vector.reciprocal(weight_inv[:, i % 2, :], by_head[:, :, D]))
                    taken(nc.vector.tensor_tensor(context[:, i, :].rearrange("p (h d) -> p h d", d=D),
                                                  by_head[:, :, 0:D],
                                                  weight_inv[:, i % 2, :].unsqueeze(2).broadcast_to([128, HEADS, D]),
                                                  ALU.mult))
                elif kind == "turn_context":
                    taken(nc.vector.tensor_copy(context_t[:, columns], frm[:, :]))
                elif kind == "combine":
                    taken(nc.vector.tensor_tensor(attended[:, blocks, :], by_token, normed_old[:, blocks, :], ALU.add))
                    if i == 1:
                        taken_by_self()
                        layer_norm(b, 0, attended, normed1).then_inc(normed1_ready, 1)
                elif kind == "features":
                    taken(nc.vector.tensor_copy(feature_t[:], frm[0:STACK, :].bitcast(BF16)))
                elif kind == "hidden":
                    taken(nc.vector.tensor_scalar(hidden[:, j, columns], frm[:, :], bias_hidden[:, j:j + 1], 0.0,
                                                  ALU.add, ALU.max))
                elif kind == "project":
                    if i == 0:
                        dve.wait_ge(x1_bias_ready, finishes(b) + 1)
                    taken(nc.vector.tensor_tensor(projected[:, blocks, :], by_token, x1_bias[:, blocks, :], ALU.add))
                    if i == 1:
                        taken_by_self()
                        layer_norm(b, 1, projected, normed2).then_inc(normed2_ready, 1)
                elif kind == "turn_tokens":
                    taken(nc.vector.tensor_copy(normed3_t[:, columns], frm[:, :]))
                elif kind == "route":
                    taken(nc.vector.tensor_tensor(
                        logits[:, blocks, :], frm[:, 0:4 * EXPERTS].rearrange("p (a e) -> p a e", a=4),
                        bias_router[:].unsqueeze(1).broadcast_to([128, 4, EXPERTS]), ALU.add))
                    if i == 1:
                        taken_by_self()
                        rank_experts()
                elif kind == "turn_gates":
                    taken(nc.vector.tensor_copy(gates_t[:], frm[0:BLOCKS * EXPERTS, 0:128]))
                elif kind == "expert_bias":
                    taken(nc.vector.tensor_tensor(mixed[:, blocks, :], by_token, x2[:, blocks, :], ALU.add))
                    if i == 1:
                        taken_by_self()
                elif kind == "expert":
                    for n in range(4):
                        expert = 4 * j + n
                        last = nc.vector.scalar_tensor_tensor(mixed[:, i, :], frm[:, 128 * n:128 * (n + 1)],
                                                              gates[:, i, expert:expert + 1], mixed[:, i, :],
                                                              ALU.mult, ALU.add)
                        if n < 3:
                            link(last)
                    taken(last)
                    taken_by_self()
                elif kind == "image":
                    if i == 0:
                        wait(dve, image_stored, 16 * finishes(b))
                    taken(nc.vector.tensor_copy(image_out[:, columns], frm[:, :]))

            def step(b):
                stages = stages_of(b)
                jobs, base, where = job_counter(b)
                done[0] = 0
                for group in range(GROUPS):
                    if group % 8 == 0 and group and "attend" in stages:
                        save_sums(b, group // 8 - 1)
                    if group == 2 and "prepare" in stages:
                        channel_moments(b)
                    if "attend" in stages and group == 16:
                        dve.wait_ge(moved_on, b + 1)
                        link(nc.vector.tensor_copy(tokens_mid[:], tokens_new[:]))
                    if "prepare" in stages:
                        if group == 34:
                            token_moments(tokens_new)
                        if group == 36:
                            normalise(b, 3 * int("finish" in stages), tokens_new, normed_new).then_inc(normed_ready, 1)
                        if group == 39:
                            dve.wait_ge(angle_ready, b + 2)
                        if 39 <= group < 39 + COSINE_PARTS:
                            cosine_part(group - 39)
                        if group in (48, 49):
                            cosine_products(group - 48)
                        if group in (50, 51, 52):
                            split_products(group - 50)
                    if "finish" in stages:
                        if group == 14:
                            dve.wait_ge(x1_ready, finishes(b) + 1)
                            link(nc.vector.tensor_copy(feature_angle[:], x1[:, :, 0:FEATURES]))
                            link(reduce_angle(feature_angle[:], feature_turns[:]))
                            half_sine(feature_angle[:], feature_turns[:], feature_cos[:])
                            link(from_half_sine(feature_angle[:], feature_turns[:], feature_cos[:]))
                            stack_features()
                        if group == 35:
                            weigh_experts(b)
                        if group == 28:
                            dve.wait_ge(x2_ready, finishes(b) + 1)
                            layer_norm(b, 2, x2, normed3).then_inc(normed3_ready, 1)
                    for at, kind, i, j, number in jobs:
                        if at == group and (kind != "conv" or j == LAST_TAPS):
                            take(b, base, stages, kind, i, j, number)
                if "attend" in stages:
                    save_sums(b, 2 * QUADS - 1)
                dve.sem_clear(vector_step)

            steps(dve, step)


def kernel(x, L0_conv_weight, L0_conv_bias, L1_attn_rx_theta, L1_attn_ry_theta, L1_attn_w_comb, L1_attn_b_comb,
           L1_attn_w1, L1_attn_b1, L1_attn_w2, L1_attn_b2, L1_attn_g1, L1_attn_beta1, L1_attn_g2, L1_attn_beta2,
           L1_ffn_router_w, L1_ffn_router_b, L1_ffn_expert_w, L1_ffn_expert_b):
    import concourse.bacc as bacc
    from concourse.bass_utils import run_bass_kernel_spmd

    def rows(row, times=1):
        return np.tile(np.asarray(row)[None, :], (128, times))

    bias_blocks = np.zeros((BLOCKS, EXPERTS, BLOCKS, C), np.float32)
    for blk in range(BLOCKS):
        bias_blocks[blk, :, blk, :] = np.asarray(L1_ffn_expert_b)

    laid_out = {
        "x": np.asarray(x).reshape(IMAGES, C, TOKENS),
        "conv_w": np.asarray(L0_conv_weight).transpose(1, 2, 3, 0).reshape(C, 9, C),
        "conv_b": np.asarray(L0_conv_bias).reshape(C, 1),
        "group_mean": np.kron(np.eye(C // GROUP_CHANNELS), np.ones((GROUP_CHANNELS, GROUP_CHANNELS))).astype(np.float32)
        / np.float32(GROUP_CHANNELS),
        "identity": np.eye(128, dtype=np.float32),
        "theta": rows(L1_attn_rx_theta, HEADS),
        "ry": rows(L1_attn_ry_theta),
        "w_comb": np.asarray(L1_attn_w_comb).T,
        "b_comb": rows(L1_attn_b_comb),
        "w1": np.asarray(L1_attn_w1).T,
        "b1": np.asarray(L1_attn_b1).reshape(CHUNKS, 128).T,
        "w2": np.asarray(L1_attn_w2).reshape(C, CHUNKS, 128).transpose(2, 1, 0),
        "b2": rows(L1_attn_b2),
        "g1": rows(L1_attn_g1),
        "beta1": rows(L1_attn_beta1),
        "g2": rows(L1_attn_g2),
        "beta2": rows(L1_attn_beta2),
        "router_w": np.asarray(L1_ffn_router_w),
        "router_b": rows(L1_ffn_router_b),
        "expert_w": np.asarray(L1_ffn_expert_w).transpose(1, 0, 2).reshape(C, EXPERTS * C),
        "expert_b": bias_blocks.reshape(BLOCKS * EXPERTS, BLOCKS, C),
        "earlier": np.tile(np.tril(np.ones((EXPERTS, EXPERTS), np.float32), -1)[None], (128, 1, 1)),
    }
    nc = bacc.Bacc("TRN2", target_bir_lowering=False, num_devices=1)
    arrays, args = {}, []
    for name, array in laid_out.items():
        array = np.ascontiguousarray(array)
        arrays[f"in_{name}"] = array
        args.append(nc.dram_tensor(f"in_{name}", array.shape, mybir.dt.from_np(array.dtype), kind="ExternalInput").ap())
    out = nc.dram_tensor("out_image", (IMAGES, C, TOKENS), F32, kind="ExternalOutput").ap()
    conv_hybrid(nc, *args, out)
    result = run_bass_kernel_spmd(nc, [arrays], core_ids=[0])
    return result.results[0]["out_image"].reshape(IMAGES, C, SIDE, SIDE)
```

```python
import math
from contextlib import ExitStack

import numpy as np
import concourse.bass as bass
from concourse import mybir

F32 = mybir.dt.float32
F16 = mybir.dt.float16
BF16 = mybir.dt.bfloat16
I32 = mybir.dt.int32
ALU = mybir.AluOpType
ACT = mybir.ActivationFunctionType
AX = mybir.AxisListType

IMAGES, C, SIDE, TOKENS = 32, 128, 32, 1024
PADDED = SIDE + 2
GROUP_CHANNELS = 4
BLOCKS = TOKENS // 128
HALF = TOKENS // 2
HEADS, D = 16, 8
QUADS = HEADS // 4
FEATURES, HIDDEN, CHUNKS = 8, 512, 4
PARTS = 3
STACK = PARTS * PARTS * FEATURES
EXPERTS, CHOSEN = 8, 2
GROUPS = QUADS * 2 * BLOCKS
PAIRS = 2 * GROUPS
RING = 4
STRIP = 32
SPLIT = 1024.0
SCORE_SCALE = 1.0 / (math.sqrt(D) * SPLIT * SPLIT)
DATA_SCALE = 512.0
WEIGHT_SCALE = 2.0 ** 14
TINY = 1e-30
EXPONENT_BITS = 0x7F800000
PAIR_PRODUCTS = ((0, 0), (0, 1), (1, 0))
ROUND = 1.5 * 2.0 ** 23
TURN_HI = 6.28125
TURN_LO = 2.0 * math.pi - 6.28125
HALF_SINE = (0.7071067781556869, -0.029462767169504807, 0.00036827228376790403,
             -2.1886103953064436e-06, 7.195782692868076e-09)
EPS = 1e-5


def schedule():
    jobs = [(3, "attend", "key", 3, v) for v in range(2)]
    jobs += [(1 + i, "finish", "context", i, 0) for i in range(BLOCKS)]
    jobs += [(4, "prepare", "mean", 0, 0), (6, "prepare", "spread", 0, 0)]
    jobs += [(9, "finish", "turn_context", i, 0) for i in range(2)]
    jobs += [(10, "finish", "combine", i, 0) for i in range(2)]
    jobs += [(11 + i, "prepare", "conv", 0, i) for i in range(3)]
    jobs += [(14 + i, "prepare", "conv", 1, i) for i in range(3)]
    jobs += [(17, "finish", "features", 0, 0)]
    jobs += [(17 + i, "prepare", "tokens", i, 0) for i in range(2)]
    jobs += [(18 + (CHUNKS * i + j + 1) // 2, "finish", "hidden", i, j) for i in range(2) for j in range(CHUNKS)]
    jobs += [(22 + i, "finish", "project", i, 0) for i in range(2)]
    jobs += [(33 + i, "finish", "turn_tokens", i, 0) for i in range(2)]
    jobs += [(35 + 2 * i + j, "finish", "route", i, j) for i in range(2) for j in range(2)]
    jobs += [(42, "finish", "turn_gates", 0, 0)]
    jobs += [(43 + i, "finish", "expert_bias", i, 0) for i in range(2)]
    jobs += [(45 + 2 * i + j, "finish", "expert", i, j) for i in range(BLOCKS) for j in range(2)]
    jobs += [(first + v, "prepare", "key", h, v) for h, first in enumerate((56, 58, 60)) for v in range(2)]
    jobs += [(61 + i, "finish", "image", i, 0) for i in range(2)]
    return sorted(jobs, key=lambda job: job[0])


JOBS = schedule()
LAST_PART = {"conv": 2, "route": 1}


def is_whole(kind, j):
    return j == LAST_PART.get(kind, j)


def numbered(stages):
    out, number = [], 0
    for group, stage, kind, i, j in JOBS:
        if stage in stages:
            out.append((group, kind, i, j, number))
            number += is_whole(kind, j)
    return out, number


STEADY = ("attend", "prepare", "finish")


def stages_of(b):
    if not isinstance(b, int):
        return STEADY
    return (("attend",) if 0 <= b < IMAGES else ()) + (("prepare",) if b + 1 < IMAGES else ()) \
        + (("finish",) if b >= 1 else ())


def before(b, count):
    if isinstance(b, int):
        return sum(count(stages_of(s)) for s in range(-1, b))
    first = count(stages_of(-1)) + count(stages_of(0))
    return (b - 1) * count(STEADY) + first


def conv_hybrid(nc, x, conv_w, conv_b, group_mean, identity, theta, ry, w_comb, b_comb, w1, b1, w2, b2,
                g1, beta1, g2, beta2, router_w, router_b, expert_w, expert_b, earlier, out):
    ctx = ExitStack()
    with ctx:
        def sb(name, shape, dtype=F32):
            return ctx.enter_context(nc.sbuf_tensor(name, shape, dtype))

        def sem(name):
            return ctx.enter_context(nc.semaphore(name))

        w_conv = sb("w_conv", [C, 2, 9, C], F16)
        bias_conv = sb("bias_conv", [C, 1])
        mean_of_group = sb("mean_of_group", [C, C])
        ident = sb("ident", [128, 128])
        ident16 = sb("ident16", [128, 128], F16)
        ident_bf16 = sb("ident_bf16", [128, 128], BF16)
        shift = sb("shift", [128, C])
        ry_angle = sb("ry_angle", [128, 3, FEATURES])
        w_combine = sb("w_combine", [C, C])
        bias_combine = sb("bias_combine", [128, C])
        w_hidden = sb("w_hidden", [STACK, HIDDEN], BF16)
        bias_hidden = sb("bias_hidden", [128, CHUNKS])
        w_project = sb("w_project", [128, CHUNKS, C])
        bias_project = sb("bias_project", [128, C])
        gain1 = sb("gain1", [128, C])
        offset1 = sb("offset1", [128, C])
        gain2 = sb("gain2", [128, C])
        offset2 = sb("offset2", [128, C])
        w_router = sb("w_router", [C, EXPERTS])
        bias_router = sb("bias_router", [128, EXPERTS])
        w_expert = sb("w_expert", [C, 2, EXPERTS * C], F16)
        bias_expert = sb("bias_expert", [BLOCKS * EXPERTS, BLOCKS, C])
        is_earlier = sb("is_earlier", [128, EXPERTS, EXPERTS])
        extremes = sb("extremes", [128, 2, 2])
        peak = sb("peak", [128, 2])
        peak_on_diagonal = sb("peak_on_diagonal", [2, 3])
        ones = sb("ones", [2, 128])
        weight_scale = sb("weight_scale", [128, 2])
        unscale = sb("unscale", [128, 2])
        minus_half = sb("minus_half", [128, BLOCKS])
        eps = sb("eps", [128, BLOCKS])

        image = sb("image", [C, TOKENS])
        pixel_stats = sb("pixel_stats", [C, 2, 6])
        channel_stats = sb("channel_stats", [C, 2])
        group_stats = sb("group_stats", [C, 4])
        group_rstd = sb("group_rstd", [C, 2])
        padded = sb("padded", [C, 2, PADDED, PADDED], F16)
        layer0 = sb("layer0", [C, TOKENS])
        tokens_new = sb("tokens_new", [128, BLOCKS, C])
        normed_new = sb("normed_new", [128, BLOCKS, C])
        scratch = sb("scratch", [128, CHUNKS, TOKENS])
        angle, turns = (scratch[:, n, :].rearrange("p (a c) -> p a c", a=BLOCKS) for n in range(2))
        cosine = scratch[:, 2, :].rearrange("p (a c) -> p a c", a=BLOCKS)
        product = sb("product", [128, BLOCKS * HEADS, D])
        key_halves = sb("key_halves", [128, BLOCKS, HEADS, 4 * D], F16)
        query_halves = sb("query_halves", [128, BLOCKS, HEADS, 4 * D], F16)

        keys = sb("keys", [128, QUADS, TOKENS], F16)
        queries = sb("queries", [128, QUADS, TOKENS], F16)
        values = sb("values", [128, BLOCKS, HEADS, STRIP])
        probs = sb("probs", [128, RING, 2 * HALF])
        sums = sb("sums", [128, QUADS, TOKENS])
        raw_conv = sums[:].rearrange("p a t -> p (a t)")[:, 0:9 * C]
        raw_expert = sums[:, 2, :]

        tokens_mid = sb("tokens_mid", [128, BLOCKS, C])
        tokens_old = sb("tokens_old", [128, BLOCKS, C])
        normed_old = sb("normed_old", [128, BLOCKS, C])
        weight_inv = sb("weight_inv", [128, 2, HEADS])
        context = sb("context", [128, BLOCKS, C])
        context_t = sb("context_t", [C, TOKENS])
        attended = sb("attended", [128, BLOCKS, C])
        normed1 = sb("normed1", [128, BLOCKS, C])
        x1 = sb("x1", [128, BLOCKS, C])
        x1_bias = sb("x1_bias", [128, BLOCKS, C])
        feature_angle = sb("feature_angle", [128, BLOCKS, FEATURES])
        feature_turns = sb("feature_turns", [128, BLOCKS, FEATURES])
        feature_cos = sb("feature_cos", [128, BLOCKS, FEATURES])
        feature = sb("feature", [128, BLOCKS, FEATURES])
        feature_part = sb("feature_part", [128, PARTS, BLOCKS, FEATURES], BF16)
        feature_stack = sb("feature_stack", [128, BLOCKS, PARTS, PARTS, FEATURES], BF16)
        feature_t = sb("feature_t", [STACK, TOKENS], BF16)
        hidden = scratch
        w_hidden_rest = scratch[0:FEATURES, 0, :].rearrange("p (a f) -> p a f", a=2)
        w_hidden_part = scratch[0:FEATURES, 1:3, :].rearrange("p a f -> p (a f)").bitcast(BF16) \
            [:, 0:PARTS * HIDDEN].rearrange("p (a f) -> p a f", a=PARTS)
        projected = attended
        normed2 = sb("normed2", [128, BLOCKS, C])
        normed3_halves = normed2[:].rearrange("p a c -> p (a c)").bitcast(F16).rearrange("p (v t) -> p v t", v=2)
        x2 = sb("x2", [128, BLOCKS, C])
        normed3, normed3_t = context, context_t
        logits = sb("logits", [128, BLOCKS, EXPERTS])
        top = sb("top", [128, BLOCKS])
        below = sb("below", [128, BLOCKS, EXPERTS])
        ahead_of = sb("ahead_of", [128, BLOCKS, EXPERTS, EXPERTS])
        tied = sb("tied", [128, BLOCKS, EXPERTS, EXPERTS])
        rank = sb("rank", [128, BLOCKS, EXPERTS])
        weight = sb("weight", [128, BLOCKS, EXPERTS])
        chosen = sb("chosen", [128, BLOCKS, EXPERTS])
        gates_unscaled = sb("gates_unscaled", [128, BLOCKS, EXPERTS])
        chosen_sum = sb("chosen_sum", [128, BLOCKS])
        chosen_inv = sb("chosen_inv", [128, BLOCKS])
        gates_wide = sb("gates_wide", [128, 2, BLOCKS, EXPERTS])
        gates = gates_wide[:, 0, :, :]
        gates_t = sb("gates_t", [BLOCKS * EXPERTS, 128])
        mixed = x2
        image_out = sb("image_out", [C, TOKENS])
        block_stats = sb("block_stats", [128, BLOCKS, 6])
        token_stats = sb("token_stats", [128, BLOCKS, 2])
        variance = sb("variance", [128, BLOCKS])
        rstd = sb("rstd", [128, BLOCKS])

        scores = [ctx.enter_context(nc.psum_tensor(f"scores{n}", [128, 2 * HALF], F32)) for n in range(2)]
        sums_acc = ctx.enter_context(nc.psum_tensor("sums_acc", [128, 2, HALF], F32))
        bank = [ctx.enter_context(nc.psum_tensor(f"bank{n}", [128, HALF], F32)) for n in range(2)]

        weights_loaded = sem("weights_loaded")
        w_hidden_split, w_hidden_stacked = sem("w_hidden_split"), sem("w_hidden_stacked")
        peaks_ready, peaks_moved = sem("peaks_ready"), sem("peaks_moved")
        weights_split = sem("weights_split")
        image_loaded = sem("image_loaded")
        filled = sem("filled")
        job_ready = sem("job_ready")
        job_taken = sem("job_taken")
        scores_ready = sem("scores_ready")
        probs_ready = sem("probs_ready")
        probs_used = sem("probs_used")
        sums_saved = sem("sums_saved")
        head_ready = sem("head_ready")
        moments_ready = sem("moments_ready")
        deviation_ready = sem("deviation_ready")
        group_rstd_ready = sem("group_rstd_ready")
        padded_ready = sem("padded_ready")
        image_biased = sem("image_biased")
        stats_ready = sem("stats_ready")
        rstd_ready = sem("rstd_ready")
        moved_on = sem("moved_on")
        normed_ready = sem("normed_ready")
        angle_ready = sem("angle_ready")
        halves_ready = sem("halves_ready")
        normed1_ready, x1_ready = sem("normed1_ready"), sem("x1_ready")
        normed2_ready, x2_ready = sem("normed2_ready"), sem("x2_ready")
        x1_bias_ready = sem("x1_bias_ready")
        feature_ready = sem("feature_ready")
        normed3_ready = sem("normed3_ready")
        below_ready, weight_ready = sem("below_ready"), sem("weight_ready")
        gates_ready = sem("gates_ready")
        image_stored = sem("image_stored")
        vector_step = sem("vector_step")
        pool_step = sem("pool_step")

        loads = [(raw_conv, conv_w), (bias_conv, conv_b), (mean_of_group, group_mean), (ident, identity),
                 (shift, theta), (ry_angle[:, 0, :], ry), (w_combine, w_comb), (bias_combine, b_comb),
                 (w_hidden_rest[:, 0, :], w1), (bias_hidden, b1), (w_project, w2), (bias_project, b2), (gain1, g1),
                 (offset1, beta1), (gain2, g2), (offset2, beta2), (w_router, router_w),
                 (bias_router, router_b), (raw_expert, expert_w), (bias_expert, expert_b),
                 (is_earlier, earlier)]
        FILLS = 9

        def everywhere(row):
            return row[:, :].unsqueeze(1).broadcast_to([128, BLOCKS, row.shape[1]])

        def finishes(b):
            return before(b, lambda stages: int("finish" in stages))

        def job_counter(b):
            jobs, _ = numbered(stages_of(b))
            base = before(b, lambda stages: numbered(stages)[1])
            where = {(kind, i, j): number for _, kind, i, j, number in jobs}
            return jobs, base, where

        def wait(engine, semaphore, value):
            if not isinstance(value, int) or value > 0:
                engine.wait_ge(semaphore, value)

        def steps(engine, body):
            body(-1)
            body(0)
            with engine.Fori(1, IMAGES - 1) as b:
                body(b)
            body(IMAGES - 1)
            body(IMAGES)

        block = ctx.enter_context(nc.Block())

        @block.sync
        def _(sp):
            for tile, source in loads:
                sp.dma_start(tile if isinstance(tile, bass.AP) else tile[:], source).then_inc(weights_loaded, 16)
            sp.wait_ge(w_hidden_split, 1)
            for pairing in range(PARTS * PARTS):
                sp.dma_start(w_hidden[FEATURES * pairing:FEATURES * (pairing + 1), :],
                             w_hidden_part[:, pairing % PARTS, :]).then_inc(w_hidden_stacked, 16)

            def step(b):
                stages = stages_of(b)
                jobs, base, where = job_counter(b)
                if "prepare" in stages:
                    wait(sp, normed_ready, b + 1)
                    sp.dma_start(image[:], x[b + 1, :, :]).then_inc(image_loaded, 16)
                if "finish" in stages:
                    wait(sp, job_taken, base + where["image", 1, 0] + 1)
                    sp.dma_start(out[b - 1, :, :], image_out[:]).then_inc(image_stored, 16)

            steps(sp, step)
            sp.wait_ge(image_stored, 16 * IMAGES)

        @block.tensor
        def _(pe):
            pe.wait_ge(weights_loaded, 16 * len(loads))
            pe.wait_ge(filled, FILLS)
            pe.wait_ge(w_hidden_stacked, 16 * PARTS * PARTS)
            pe.wait_ge(peaks_ready, 1)
            nc.tensor.matmul(bank[0][0:2, 0:128], peak[:], ident[:], start=True, stop=True).then_inc(peaks_moved, 1)
            pe.wait_ge(peaks_ready, 2)
            nc.tensor.matmul(bank[1][:, 0:2], ones[:], peak_on_diagonal[:, 0:2], start=True,
                             stop=True).then_inc(peaks_moved, 1)
            pe.wait_ge(weights_split, 2)

            def score_pair(b, group, pair):
                quad, half, blk = group // 16, group // 8 % 2, group % 8
                wait(pe, probs_ready, b * PAIRS + 2 * group + pair - 1)
                for n in range(2):
                    head = 2 * pair + n
                    rows = slice(STRIP * head, STRIP * (head + 1))
                    last = nc.tensor.matmul(scores[pair][:, n * HALF:(n + 1) * HALF],
                                            keys[rows, quad, 128 * blk:128 * (blk + 1)],
                                            queries[rows, quad, half * HALF:(half + 1) * HALF],
                                            start=True, stop=True)
                last.then_inc(scores_ready, 1)

            def first_scores(b):
                pe.wait_ge(head_ready, b * QUADS + 1)
                score_pair(b, 0, 0)
                score_pair(b, 0, 1)

            def sum_group(b, group):
                quad, half, blk = group // 16, group // 8 % 2, group % 8
                unit = 2 * quad + half
                if blk == 0:
                    wait(pe, sums_saved, b * 2 * QUADS + unit - 1)
                pe.wait_ge(probs_ready, b * PAIRS + 2 * group + 2)
                for head in range(4):
                    pair = 2 * group + head // 2
                    last = nc.tensor.matmul(sums_acc[STRIP * head:STRIP * (head + 1), half, :],
                                            values[:, blk, 4 * quad + head, :],
                                            probs[:, pair % RING, (head % 2) * HALF:(head % 2 + 1) * HALF],
                                            start=(blk == 0), stop=(blk == BLOCKS - 1))
                last.then_inc(probs_used, 1)

            def job(b, base, where, kind, i, j, number):
                to = bank[number % 2]

                def taken(*which):
                    pe.wait_ge(job_taken, base + where[which] + 1)

                if kind not in LAST_PART or j == 0:
                    wait(pe, job_taken, base + number - 1)
                if kind == "mean":
                    pe.wait_ge(moments_ready, b + 2)
                    last = nc.tensor.matmul(to[:, 0:1], mean_of_group[:], channel_stats[:, 0:1], start=True, stop=True)
                elif kind == "spread":
                    pe.wait_ge(deviation_ready, b + 2)
                    last = nc.tensor.matmul(to[:, 0:1], mean_of_group[:], group_stats[:, 2:3], start=True, stop=True)
                elif kind == "conv":
                    if j == 0:
                        pe.wait_ge(padded_ready, b + 2)
                    for tap in range(3 * j, 3 * j + 3):
                        row = i * SIDE // 2 + tap // 3
                        for of_weight, of_data in PAIR_PRODUCTS:
                            last = nc.tensor.matmul(to[:, :], w_conv[:, of_weight, tap, :],
                                                    padded[:, of_data, row:row + SIDE // 2, tap % 3:tap % 3 + SIDE],
                                                    start=(tap == 0 and of_weight + of_data == 0),
                                                    stop=(tap == 8 and of_weight == 1))
                elif kind in ("tokens", "turn_context", "turn_tokens", "image"):
                    if kind == "tokens":
                        taken("conv", i, LAST_PART["conv"])
                    elif kind == "turn_context":
                        taken("context", 4 * i + 3, 0)
                    elif kind == "turn_tokens":
                        pe.wait_ge(normed3_ready, finishes(b) + 1)
                    else:
                        taken("expert", 4 * i + 3, 1)
                    source = {"turn_context": context, "turn_tokens": normed3, "image": mixed}
                    for n in range(4):
                        blk = 4 * i + n
                        piece = layer0[:, 128 * blk:128 * (blk + 1)] if kind == "tokens" else source[kind][:, blk, :]
                        last = nc.tensor.transpose(to[:, 128 * n:128 * (n + 1)], piece, ident[:])
                elif kind == "key":
                    of_next = 0 if i == QUADS - 1 else 1
                    pe.wait_ge(halves_ready, b + 1 + of_next)
                    for blk in range(BLOCKS):
                        piece = (query_halves if j else key_halves)[:, blk, 4 * i:4 * i + 4, :]
                        last = nc.tensor.transpose(to[:, :].bitcast(F16)[:, 128 * blk:128 * (blk + 1)],
                                                   piece.rearrange("p h d -> p (h d)"), ident16[:])
                elif kind == "context":
                    if i == 0:
                        pe.wait_ge(sums_saved, b * 2 * QUADS)
                    for quad in range(QUADS):
                        last = nc.tensor.transpose(to[:, 128 * quad:128 * (quad + 1)],
                                                   sums[:, quad, 128 * i:128 * (i + 1)], ident[:])
                elif kind == "combine":
                    taken("turn_context", i, 0)
                    for n in range(4):
                        last = nc.tensor.matmul(to[:, 128 * n:128 * (n + 1)],
                                                context_t[:, 128 * (4 * i + n):128 * (4 * i + n + 1)],
                                                w_combine[:], start=True, stop=True)
                elif kind == "features":
                    pe.wait_ge(feature_ready, finishes(b) + 1)
                    for blk in range(BLOCKS):
                        last = nc.tensor.transpose(to[0:STACK, :].bitcast(BF16)[:, 128 * blk:128 * (blk + 1)],
                                                   feature_stack[:, blk, :, :, :].rearrange("p a b f -> p (a b f)"),
                                                   ident_bf16[:])
                elif kind == "turn_gates":
                    pe.wait_ge(gates_ready, finishes(b) + 1)
                    last = nc.tensor.transpose(to[:, 0:128], gates_wide[:].rearrange("p z a e -> p (z a e)"), ident[:])
                elif kind == "hidden":
                    taken("features", 0, 0)
                    last = nc.tensor.matmul(to[:, :], w_hidden[:, 128 * j:128 * (j + 1)],
                                            feature_t[:, i * HALF:(i + 1) * HALF], start=True, stop=True)
                elif kind == "project":
                    taken("hidden", i, CHUNKS - 1)
                    for n in range(4):
                        at = 128 * (4 * i + n)
                        for chunk in range(CHUNKS):
                            last = nc.tensor.matmul(to[:, 128 * n:128 * (n + 1)], hidden[:, chunk, at:at + 128],
                                                    w_project[:, chunk, :],
                                                    start=(chunk == 0), stop=(chunk == CHUNKS - 1))
                elif kind == "route":
                    taken("turn_tokens", i, 0)
                    for n in range(2 * j, 2 * j + 2):
                        last = nc.tensor.matmul(to[:, EXPERTS * n:EXPERTS * (n + 1)],
                                                normed3_t[:, 128 * (4 * i + n):128 * (4 * i + n + 1)],
                                                w_router[:], start=True, stop=True)
                elif kind == "expert_bias":
                    taken("turn_gates", 0, 0)
                    last = nc.tensor.matmul(to[:, :], gates_t[:],
                                            bias_expert[:, 4 * i:4 * i + 4, :].rearrange("p a c -> p (a c)"),
                                            start=True, stop=True)
                elif kind == "expert":
                    for of_data, of_weight in PAIR_PRODUCTS:
                        last = nc.tensor.matmul(to[:, :], normed3_halves[:, of_data, 128 * i:128 * (i + 1)],
                                                w_expert[:, of_weight, j * HALF:(j + 1) * HALF],
                                                start=(of_data + of_weight == 0), stop=(of_data == 1))
                if is_whole(kind, j):
                    last.then_inc(job_ready, 1)

            def step(b):
                stages = stages_of(b)
                jobs, base, where = job_counter(b)
                for group in range(GROUPS):
                    if "attend" in stages:
                        if group + 1 < GROUPS:
                            if (group + 1) % 16 == 0:
                                pe.wait_ge(head_ready, b * QUADS + (group + 1) // 16 + 1)
                            score_pair(b, group + 1, 0)
                            score_pair(b, group + 1, 1)
                        elif "prepare" in stages:
                            first_scores(b + 1)
                        sum_group(b, group)
                    for at, kind, i, j, number in jobs:
                        if at == group:
                            job(b, base, where, kind, i, j, number)
                if "attend" not in stages and "prepare" in stages:
                    first_scores(b + 1)

            steps(pe, step)

        @block.scalar
        def _(act):
            def gate_exponentials(b):
                act.wait_ge(below_ready, finishes(b) + 1)
                nc.scalar.activation(weight[:], below[:], ACT.Exp).then_inc(weight_ready, 1)

            def step(b):
                stages = stages_of(b)
                for pair in range(PAIRS):
                    if "attend" in stages:
                        act.wait_ge(scores_ready, b * PAIRS + pair + 1)
                        if pair % 2 == 0:
                            wait(act, probs_used, b * GROUPS + pair // 2 - RING // 2 + 1)
                        nc.scalar.activation(probs[:, pair % RING, :], scores[pair % 2][:, :], ACT.Exp,
                                             scale=SCORE_SCALE).then_inc(probs_ready, 1)
                    if pair == 2 * 40 and "finish" in stages:
                        gate_exponentials(b)

            steps(act, step)

        @block.gpsimd
        def _(pool):
            nc.gpsimd.memset(minus_half[:], -0.5).then_inc(filled, 1)
            nc.gpsimd.memset(eps[:], EPS).then_inc(filled, 1)
            nc.gpsimd.memset(padded[:], 0.0).then_inc(filled, 1)
            nc.gpsimd.memset(ones[:], 1.0).then_inc(filled, 1)
            pool.wait_ge(filled, FILLS)
            pool.wait_ge(weights_loaded, 16 * len(loads))
            done = [0]

            def link(instruction):
                instruction.then_inc(pool_step, 1)
                done[0] += 1
                pool.wait_ge(pool_step, done[0])

            def layer_rstd(b, n):
                base = before(b, lambda stages: ("prepare" in stages) + 3 * ("finish" in stages))
                pool.wait_ge(stats_ready, base + n + 1)
                link(nc.gpsimd.tensor_tensor(variance[:], token_stats[:, :, 1], eps[:], ALU.add))
                nc.gpsimd.tensor_tensor(rstd[:], variance[:], minus_half[:], ALU.pow).then_inc(rstd_ready, 1)

            def step(b):
                stages = stages_of(b)
                jobs, base, where = job_counter(b)
                done[0] = 0
                n = 0
                if "prepare" in stages:
                    pool.wait_ge(job_taken, base + where["spread", 0, 0] + 1)
                    link(nc.gpsimd.tensor_tensor(group_rstd[:, 0:1], group_stats[:, 3:4], eps[:, 0:1], ALU.add))
                    nc.gpsimd.tensor_tensor(group_rstd[:, 1:2], group_rstd[:, 0:1], minus_half[:, 0:1],
                                            ALU.pow).then_inc(group_rstd_ready, 1)
                    pool.wait_ge(padded_ready, b + 2)
                    nc.gpsimd.tensor_tensor(image[:], image[:], bias_conv[:, 0:1].broadcast_to([C, TOKENS]),
                                            ALU.add).then_inc(image_biased, 1)
                if "finish" in stages:
                    layer_rstd(b, n)
                    n += 1
                    pool.wait_ge(normed1_ready, finishes(b) + 1)
                    link(nc.gpsimd.tensor_tensor(normed1[:], normed1[:], everywhere(gain1), ALU.mult))
                    nc.gpsimd.tensor_tensor(x1[:], normed1[:], everywhere(offset1), ALU.add).then_inc(x1_ready, 1)
                    pool.wait_ge(x1_ready, finishes(b) + 1)
                    nc.gpsimd.tensor_tensor(x1_bias[:], x1[:], everywhere(bias_project),
                                            ALU.add).then_inc(x1_bias_ready, 1)
                    nc.gpsimd.tensor_tensor(tokens_old[:], tokens_mid[:], everywhere(offset2), ALU.add)
                if "attend" in stages:
                    wait(pool, normed_ready, b + 1)
                    nc.gpsimd.tensor_tensor(normed_old[:], normed_new[:], everywhere(bias_combine),
                                            ALU.add).then_inc(moved_on, 1)
                if "prepare" in stages:
                    layer_rstd(b, n)
                    n += 1
                if "finish" in stages:
                    layer_rstd(b, n)
                    n += 1
                if "finish" in stages:
                    pool.wait_ge(normed2_ready, finishes(b) + 1)
                    link(nc.gpsimd.tensor_tensor(normed2[:], normed2[:], everywhere(gain2), ALU.mult))
                    nc.gpsimd.tensor_tensor(x2[:], normed2[:], tokens_old[:], ALU.add).then_inc(x2_ready, 1)
                    layer_rstd(b, n)
                if "prepare" in stages:
                    pool.wait_ge(normed_ready, b + 2)
                    nc.gpsimd.tensor_tensor(angle, normed_new[:], everywhere(shift), ALU.add).then_inc(angle_ready, 1)
                pool.sem_clear(pool_step)

            steps(pool, step)

        @block.vector
        def _(dve):
            done = [0]

            def link(instruction):
                instruction.then_inc(vector_step, 1)
                done[0] += 1
                dve.wait_ge(vector_step, done[0])

            def reduce_angle(w, turn):
                link(nc.vector.tensor_scalar(turn, w, 1.0 / (2.0 * math.pi), ROUND, ALU.mult, ALU.add))
                link(nc.vector.tensor_scalar(turn, turn, ROUND, None, ALU.subtract))
                link(nc.vector.scalar_tensor_tensor(w, turn, -TURN_HI, w, ALU.mult, ALU.add))
                return nc.vector.scalar_tensor_tensor(w, turn, -TURN_LO, w, ALU.mult, ALU.add)

            def half_sine(w, square, to):
                link(nc.vector.tensor_tensor(square, w, w, ALU.mult))
                link(nc.vector.tensor_scalar(to, square, HALF_SINE[-1], None, ALU.mult))
                for coefficient in HALF_SINE[-2:0:-1]:
                    link(nc.vector.scalar_tensor_tensor(to, to, coefficient, square, ALU.add, ALU.mult))

            def from_half_sine(w, square, to):
                link(nc.vector.scalar_tensor_tensor(w, to, HALF_SINE[0], w, ALU.add, ALU.mult))
                link(nc.vector.tensor_tensor(square, w, w, ALU.mult))
                return nc.vector.tensor_scalar(to, square, -1.0, 1.0, ALU.mult, ALU.add)

            def split(whole, parts, rest):
                link(nc.vector.tensor_copy(parts[0], whole))
                link(nc.vector.tensor_tensor(rest, whole, parts[0], ALU.subtract))
                link(nc.vector.tensor_copy(parts[1], rest))
                link(nc.vector.tensor_tensor(rest, rest, parts[1], ALU.subtract))
                return nc.vector.tensor_copy(parts[2], rest)

            nc.vector.memset(gates_wide[:, 1, :, :], 0.0).then_inc(filled, 1)
            nc.vector.memset(values[:, :, :, D + 1:STRIP], 0.0).then_inc(filled, 1)
            nc.vector.memset(values[:, :, :, D:D + 1], 1.0).then_inc(filled, 1)
            dve.wait_ge(weights_loaded, 16 * len(loads))
            nc.vector.tensor_copy(ident16[:], ident[:]).then_inc(filled, 1)
            nc.vector.tensor_copy(ident_bf16[:], ident[:]).then_inc(filled, 1)
            split(w_hidden_rest[:, 0, :], [w_hidden_part[:, n, :] for n in range(PARTS)],
                  w_hidden_rest[:, 1, :]).then_inc(w_hidden_split, 1)
            link(reduce_angle(ry_angle[:, 0, :], ry_angle[:, 1, :]))
            half_sine(ry_angle[:, 0, :], ry_angle[:, 1, :], ry_angle[:, 2, :])
            link(from_half_sine(ry_angle[:, 0, :], ry_angle[:, 1, :], ry_angle[:, 2, :]))
            cos_ry = ry_angle[:, 2, :]
            dve.wait_ge(filled, FILLS)
            for n, raw in enumerate((raw_conv, raw_expert)):
                link(nc.vector.tensor_reduce(extremes[:, n, 0:1], raw, axis=AX.X, op=ALU.max))
                link(nc.vector.tensor_reduce(extremes[:, n, 1:2], raw, axis=AX.X, op=ALU.min))
            nc.vector.scalar_tensor_tensor(peak[:], extremes[:, :, 1], -1.0, extremes[:, :, 0],
                                           ALU.mult, ALU.max).then_inc(peaks_ready, 1)
            dve.wait_ge(peaks_moved, 1)
            link(nc.vector.tensor_reduce(peak_on_diagonal[:, 2:3], bank[0][0:2, 0:128], axis=AX.X, op=ALU.max))
            nc.vector.tensor_scalar(peak_on_diagonal[:, 0:2], ident[0:2, 0:2], peak_on_diagonal[:, 2:3], None,
                                    ALU.mult).then_inc(peaks_ready, 1)
            dve.wait_ge(peaks_moved, 2)
            link(nc.vector.tensor_scalar(peak[:], bank[1][:, 0:2], TINY, None, ALU.max))
            link(nc.vector.tensor_scalar(peak[:].bitcast(I32), peak[:].bitcast(I32), EXPONENT_BITS, None,
                                         ALU.bitwise_and))
            link(nc.vector.reciprocal(weight_scale[:], peak[:]))
            link(nc.vector.tensor_scalar(weight_scale[:], weight_scale[:], WEIGHT_SCALE, None, ALU.mult))
            link(nc.vector.tensor_scalar(unscale[:], peak[:], 1.0 / (WEIGHT_SCALE * DATA_SCALE), None, ALU.mult))
            for n, (raw, halves) in enumerate(((raw_conv, w_conv[:].rearrange("p v t c -> p v (t c)")),
                                               (raw_expert, w_expert[:]))):
                link(nc.vector.tensor_scalar(halves[:, 0, :], raw, weight_scale[:, n:n + 1], None, ALU.mult))
                nc.vector.scalar_tensor_tensor(halves[:, 1, :], raw, weight_scale[:, n:n + 1], halves[:, 0, :],
                                               ALU.mult, ALU.subtract).then_inc(weights_split, 1)
            dve.wait_ge(weights_split, 2)
            dve.wait_ge(w_hidden_stacked, 16 * PARTS * PARTS)
            dve.sem_clear(vector_step)

            def channel_moments(b):
                dve.wait_ge(image_loaded, 16 * (b + 2))
                nc.vector.bn_stats(pixel_stats[:, 0, :], image[:, 0:HALF])
                link(nc.vector.bn_stats(pixel_stats[:, 1, :], image[:, HALF:TOKENS]))
                nc.vector.bn_aggr(channel_stats[:], pixel_stats[:].rearrange("p a s -> p (a s)")).then_inc(moments_ready, 1)

            def normalise_image(b):
                dve.wait_ge(group_rstd_ready, b + 2)
                link(nc.vector.tensor_scalar(layer0[:], image[:], group_stats[:, 0:1], group_rstd[:, 1:2],
                                             ALU.subtract, ALU.mult))
                by_row = layer0[:].rearrange("p (r c) -> p r c", c=SIDE)
                high, low = (padded[:, n, 1:SIDE + 1, 1:SIDE + 1] for n in range(2))
                link(nc.vector.tensor_scalar(high, by_row, DATA_SCALE, None, ALU.mult))
                nc.vector.scalar_tensor_tensor(low, by_row, DATA_SCALE, high, ALU.mult,
                                               ALU.subtract).then_inc(padded_ready, 1)

            def token_moments(source):
                for blk in range(BLOCKS - 1):
                    nc.vector.bn_stats(block_stats[:, blk, :], source[:, blk, :])
                link(nc.vector.bn_stats(block_stats[:, BLOCKS - 1, :], source[:, BLOCKS - 1, :]))
                for blk in range(BLOCKS):
                    last = nc.vector.bn_aggr(token_stats[:, blk, :], block_stats[:, blk, :])
                last.then_inc(stats_ready, 1)

            def normalise(b, n, source, target):
                base = before(b, lambda stages: ("prepare" in stages) + 3 * ("finish" in stages))
                dve.wait_ge(rstd_ready, base + n + 1)
                for blk in range(BLOCKS):
                    last = nc.vector.tensor_scalar(target[:, blk, :], source[:, blk, :], token_stats[:, blk, 0:1],
                                                   rstd[:, blk:blk + 1], ALU.subtract, ALU.mult)
                return last

            def layer_norm(b, n, source, target):
                token_moments(source)
                return normalise(b, n, source, target)

            def stack_features():
                link(nc.vector.tensor_tensor(feature[:], feature_cos[:],
                                             cos_ry.unsqueeze(1).broadcast_to([128, BLOCKS, FEATURES]), ALU.mult))
                link(split(feature[:], [feature_part[:, n, :, :] for n in range(PARTS)], feature_turns[:]))
                for n in range(PARTS):
                    last = nc.vector.tensor_copy(
                        feature_stack[:, :, n, :, :],
                        feature_part[:, n, :, :].unsqueeze(2).broadcast_to([128, BLOCKS, PARTS, FEATURES]))
                last.then_inc(feature_ready, 1)

            LAST_NORM = 3
            COSINE_GROUPS = (34, 35, 36, 37, 40, 41, 42, 43, 44)

            def cosine_part(part):
                w, square, to = angle, turns, cosine
                if part == 0:
                    link(nc.vector.tensor_scalar(turns, w, 1.0 / (2.0 * math.pi), ROUND, ALU.mult, ALU.add))
                    link(nc.vector.tensor_scalar(turns, turns, ROUND, None, ALU.subtract))
                elif part == 1:
                    link(nc.vector.scalar_tensor_tensor(w, turns, -TURN_HI, w, ALU.mult, ALU.add))
                elif part == 2:
                    link(nc.vector.scalar_tensor_tensor(w, turns, -TURN_LO, w, ALU.mult, ALU.add))
                elif part == 3:
                    link(nc.vector.tensor_tensor(square, w, w, ALU.mult))
                    link(nc.vector.tensor_scalar(to, square, HALF_SINE[4], None, ALU.mult))
                elif part < 7:
                    link(nc.vector.scalar_tensor_tensor(to, to, HALF_SINE[7 - part], square, ALU.add, ALU.mult))
                elif part == 7:
                    link(nc.vector.scalar_tensor_tensor(w, to, HALF_SINE[0], w, ALU.add, ALU.mult))
                else:
                    link(nc.vector.tensor_tensor(square, w, w, ALU.mult))
                    link(nc.vector.tensor_scalar(to, square, -1.0, 1.0, ALU.mult, ALU.add))

            def cosine_products(part):
                by_head = scratch[:, 2, :].rearrange("p (h d) -> p h d", d=D)
                cos = [by_head[:, :, d] for d in range(D)]
                if part == 0:
                    nc.vector.tensor_tensor(product[:, :, 0], cos[1], cos[2], ALU.mult)
                    link(nc.vector.tensor_tensor(product[:, :, 1], cos[0], cos[1], ALU.mult))
                for d in range(2, 5) if part == 0 else range(5, D):
                    if d + 1 < D:
                        nc.vector.tensor_tensor(product[:, :, 0], product[:, :, 0], cos[d + 1], ALU.mult)
                    link(nc.vector.tensor_tensor(product[:, :, d], product[:, :, d - 1], cos[d], ALU.mult))

            def split_products(part):
                as_keys = key_halves[:].rearrange("p a h (r d) -> p (a h) r d", r=4)
                as_queries = query_halves[:].rearrange("p a h (r d) -> p (a h) r d", r=4)
                if part == 0:
                    link(nc.vector.tensor_scalar(as_keys[:, :, 0, :], product[:], SPLIT, None, ALU.mult))
                    link(nc.vector.scalar_tensor_tensor(as_keys[:, :, 1, :], product[:], SPLIT, as_keys[:, :, 0, :],
                                                        ALU.mult, ALU.subtract))
                elif part == 1:
                    nc.vector.tensor_copy(as_keys[:, :, 2:4, :], as_keys[:, :, 0:2, :])
                    nc.vector.tensor_copy(as_queries[:, :, 2, :], as_keys[:, :, 1, :])
                else:
                    nc.vector.tensor_copy(as_queries[:, :, 0:2, :], as_keys[:, :, 0:2, :])
                    nc.vector.tensor_copy(as_queries[:, :, 3, :], as_keys[:, :, 0, :]).then_inc(halves_ready, 1)

            gate_shape = [128, BLOCKS, EXPERTS]

            def rank_experts():
                all_pairs = [128, BLOCKS, EXPERTS, EXPERTS]
                link(nc.vector.tensor_reduce(top[:], logits[:], axis=AX.X, op=ALU.max))
                nc.vector.tensor_tensor(below[:], logits[:], top[:].unsqueeze(2).broadcast_to(gate_shape),
                                        ALU.subtract).then_inc(below_ready, 1)
                other, own = (logits[:].unsqueeze(2).broadcast_to(all_pairs),
                              logits[:].unsqueeze(3).broadcast_to(all_pairs))
                nc.vector.tensor_tensor(ahead_of[:], other, own, ALU.is_gt)
                link(nc.vector.tensor_tensor(tied[:], other, own, ALU.is_equal))
                link(nc.vector.tensor_tensor(tied[:], tied[:], is_earlier[:].unsqueeze(1).broadcast_to(all_pairs),
                                             ALU.mult))
                link(nc.vector.tensor_tensor(ahead_of[:], ahead_of[:], tied[:], ALU.add))
                link(nc.vector.tensor_reduce(rank[:], ahead_of[:], axis=AX.X, op=ALU.add))

            def weigh_experts(b):
                dve.wait_ge(weight_ready, finishes(b) + 1)
                link(nc.vector.scalar_tensor_tensor(chosen[:], rank[:], float(CHOSEN), weight[:], ALU.is_lt, ALU.mult))
                link(nc.vector.tensor_reduce(chosen_sum[:], chosen[:], axis=AX.X, op=ALU.add))
                link(nc.vector.reciprocal(chosen_inv[:], chosen_sum[:]))
                nc.vector.tensor_tensor(gates, chosen[:], chosen_inv[:].unsqueeze(2).broadcast_to(gate_shape),
                                        ALU.mult).then_inc(gates_ready, 1)
                dve.wait_ge(gates_ready, finishes(b) + 1)
                link(nc.vector.tensor_scalar(gates_unscaled[:], gates, unscale[:, 1:2], None, ALU.mult))

            def save_sums(b, unit):
                quad, half = unit // 2, unit % 2
                dve.wait_ge(probs_used, b * GROUPS + BLOCKS * (unit + 1))
                nc.vector.tensor_copy(sums[:, quad, half * HALF:(half + 1) * HALF],
                                      sums_acc[:, half, :]).then_inc(sums_saved, 1)

            def take(b, base, stages, kind, i, j, number):
                frm = bank[number % 2]
                by_token = frm[:, :].rearrange("p (a c) -> p a c", a=4)
                blocks = slice(4 * i, 4 * i + 4)
                columns = slice(i * HALF, (i + 1) * HALF)

                def taken(instruction):
                    instruction.then_inc(job_taken, 1)

                def taken_by_self():
                    dve.wait_ge(job_taken, base + number + 1)

                dve.wait_ge(job_ready, base + number + 1)
                if kind == "mean":
                    taken(nc.vector.tensor_copy(group_stats[:, 0:1], frm[:, 0:1]))
                    taken_by_self()
                    link(nc.vector.tensor_tensor(group_stats[:, 1:2], channel_stats[:, 0:1], group_stats[:, 0:1],
                                                 ALU.subtract))
                    nc.vector.scalar_tensor_tensor(group_stats[:, 2:3], group_stats[:, 1:2], group_stats[:, 1:2],
                                                   channel_stats[:, 1:2], ALU.mult, ALU.add).then_inc(deviation_ready, 1)
                elif kind == "spread":
                    taken(nc.vector.tensor_copy(group_stats[:, 3:4], frm[:, 0:1]))
                    normalise_image(b)
                elif kind == "conv":
                    if i == 0:
                        dve.wait_ge(image_biased, b + 2)
                    taken(nc.vector.scalar_tensor_tensor(layer0[:, columns], frm[:, :], unscale[:, 0:1],
                                                         image[:, columns], ALU.mult, ALU.add))
                elif kind == "tokens":
                    taken(nc.vector.tensor_copy(tokens_new[:, blocks, :], by_token))
                    if i == 1:
                        taken_by_self()
                elif kind == "key":
                    taken(nc.vector.tensor_copy((queries if j else keys)[:, i, :], frm[:, :].bitcast(F16)))
                    if j == 1:
                        nc.vector.tensor_copy(values[:, :, 4 * i:4 * i + 4, 0:D],
                                              product[:].rearrange("p (a h) d -> p a h d", a=BLOCKS)
                                              [:, :, 4 * i:4 * i + 4, :]).then_inc(head_ready, 1)
                elif kind == "context":
                    by_head = frm[:, :].rearrange("p (h s) -> p h s", s=STRIP)
                    link(nc.vector.reciprocal(weight_inv[:, i % 2, :], by_head[:, :, D]))
                    taken(nc.vector.tensor_tensor(context[:, i, :].rearrange("p (h d) -> p h d", d=D),
                                                  by_head[:, :, 0:D],
                                                  weight_inv[:, i % 2, :].unsqueeze(2).broadcast_to([128, HEADS, D]),
                                                  ALU.mult))
                elif kind == "turn_context":
                    taken(nc.vector.tensor_copy(context_t[:, columns], frm[:, :]))
                elif kind == "combine":
                    taken(nc.vector.tensor_tensor(attended[:, blocks, :], by_token, normed_old[:, blocks, :], ALU.add))
                    if i == 1:
                        taken_by_self()
                        layer_norm(b, 0, attended, normed1).then_inc(normed1_ready, 1)
                elif kind == "features":
                    taken(nc.vector.tensor_copy(feature_t[:], frm[0:STACK, :].bitcast(BF16)))
                elif kind == "hidden":
                    taken(nc.vector.tensor_scalar(hidden[:, j, columns], frm[:, :], bias_hidden[:, j:j + 1], 0.0,
                                                  ALU.add, ALU.max))
                elif kind == "project":
                    if i == 0:
                        dve.wait_ge(x1_bias_ready, finishes(b) + 1)
                    taken(nc.vector.tensor_tensor(projected[:, blocks, :], by_token, x1_bias[:, blocks, :], ALU.add))
                    if i == 1:
                        taken_by_self()
                        layer_norm(b, LAST_NORM - int("prepare" not in stages) - 1, projected, normed2).then_inc(normed2_ready, 1)
                elif kind == "turn_tokens":
                    high, low = (normed3_halves[:, n, columns] for n in range(2))
                    nc.vector.tensor_copy(normed3_t[:, columns], frm[:, :])
                    link(nc.vector.tensor_scalar(high, frm[:, :], DATA_SCALE, None, ALU.mult))
                    taken(nc.vector.scalar_tensor_tensor(low, frm[:, :], DATA_SCALE, high, ALU.mult, ALU.subtract))
                elif kind == "route":
                    taken(nc.vector.tensor_tensor(
                        logits[:, blocks, :], frm[:, 0:4 * EXPERTS].rearrange("p (a e) -> p a e", a=4),
                        bias_router[:].unsqueeze(1).broadcast_to([128, 4, EXPERTS]), ALU.add))
                    if i == 1:
                        taken_by_self()
                        rank_experts()
                elif kind == "turn_gates":
                    taken(nc.vector.tensor_copy(gates_t[:], frm[0:BLOCKS * EXPERTS, 0:128]))
                elif kind == "expert_bias":
                    taken(nc.vector.tensor_tensor(mixed[:, blocks, :], by_token, x2[:, blocks, :], ALU.add))
                    if i == 1:
                        taken_by_self()
                elif kind == "expert":
                    for n in range(4):
                        expert = 4 * j + n
                        last = nc.vector.scalar_tensor_tensor(mixed[:, i, :], frm[:, 128 * n:128 * (n + 1)],
                                                              gates_unscaled[:, i, expert:expert + 1], mixed[:, i, :],
                                                              ALU.mult, ALU.add)
                        if n < 3:
                            link(last)
                    taken(last)
                    taken_by_self()
                elif kind == "image":
                    if i == 0:
                        wait(dve, image_stored, 16 * finishes(b))
                    taken(nc.vector.tensor_copy(image_out[:, columns], frm[:, :]))

            def step(b):
                stages = stages_of(b)
                jobs, base, where = job_counter(b)
                done[0] = 0
                for group in range(GROUPS):
                    if group % 8 == 0 and group and "attend" in stages:
                        save_sums(b, group // 8 - 1)
                    if group == 2 and "prepare" in stages:
                        channel_moments(b)
                    if "attend" in stages and group == 16:
                        dve.wait_ge(moved_on, b + 1)
                        link(nc.vector.tensor_copy(tokens_mid[:], tokens_new[:]))
                    if "prepare" in stages:
                        if group == 22:
                            token_moments(tokens_new)
                        if group == 23:
                            normalise(b, int("finish" in stages), tokens_new, normed_new).then_inc(normed_ready, 1)
                        if group == 34:
                            dve.wait_ge(angle_ready, b + 2)
                        if group in COSINE_GROUPS:
                            cosine_part(COSINE_GROUPS.index(group))
                        if group in (45, 46):
                            cosine_products(group - 45)
                        if group in (48, 50, 52):
                            split_products((group - 48) // 2)
                    if "finish" in stages:
                        if group == 14:
                            dve.wait_ge(x1_ready, finishes(b) + 1)
                            link(nc.vector.tensor_copy(feature_angle[:], x1[:, :, 0:FEATURES]))
                            link(reduce_angle(feature_angle[:], feature_turns[:]))
                            half_sine(feature_angle[:], feature_turns[:], feature_cos[:])
                            link(from_half_sine(feature_angle[:], feature_turns[:], feature_cos[:]))
                            stack_features()
                        if group == 41:
                            weigh_experts(b)
                        if group == 28:
                            dve.wait_ge(x2_ready, finishes(b) + 1)
                            token_moments(x2)
                        if group == 29:
                            normalise(b, LAST_NORM - int("prepare" not in stages), x2,
                                      normed3).then_inc(normed3_ready, 1)
                    for at, kind, i, j, number in jobs:
                        if at == group and is_whole(kind, j):
                            take(b, base, stages, kind, i, j, number)
                if "attend" in stages:
                    save_sums(b, 2 * QUADS - 1)
                dve.sem_clear(vector_step)

            steps(dve, step)


def kernel(x, L0_conv_weight, L0_conv_bias, L1_attn_rx_theta, L1_attn_ry_theta, L1_attn_w_comb, L1_attn_b_comb,
           L1_attn_w1, L1_attn_b1, L1_attn_w2, L1_attn_b2, L1_attn_g1, L1_attn_beta1, L1_attn_g2, L1_attn_beta2,
           L1_ffn_router_w, L1_ffn_router_b, L1_ffn_expert_w, L1_ffn_expert_b):
    import concourse.bacc as bacc
    from concourse.bass_utils import run_bass_kernel_spmd

    def rows(row, times=1):
        return np.tile(np.asarray(row)[None, :], (128, times))

    bias_blocks = np.zeros((BLOCKS, EXPERTS, BLOCKS, C), np.float32)
    for blk in range(BLOCKS):
        bias_blocks[blk, :, blk, :] = np.asarray(L1_ffn_expert_b)

    laid_out = {
        "x": np.asarray(x).reshape(IMAGES, C, TOKENS),
        "conv_w": np.asarray(L0_conv_weight).transpose(1, 2, 3, 0).reshape(C, 9 * C),
        "conv_b": np.asarray(L0_conv_bias).reshape(C, 1),
        "group_mean": np.kron(np.eye(C // GROUP_CHANNELS), np.ones((GROUP_CHANNELS, GROUP_CHANNELS))).astype(np.float32)
        / np.float32(GROUP_CHANNELS),
        "identity": np.eye(128, dtype=np.float32),
        "theta": rows(L1_attn_rx_theta, HEADS),
        "ry": rows(L1_attn_ry_theta),
        "w_comb": np.asarray(L1_attn_w_comb).T,
        "b_comb": rows(L1_attn_b_comb),
        "w1": np.asarray(L1_attn_w1).T,
        "b1": np.asarray(L1_attn_b1).reshape(CHUNKS, 128).T,
        "w2": np.asarray(L1_attn_w2).reshape(C, CHUNKS, 128).transpose(2, 1, 0),
        "b2": rows(L1_attn_b2),
        "g1": rows(L1_attn_g1),
        "beta1": rows(L1_attn_beta1),
        "g2": rows(L1_attn_g2),
        "beta2": rows(L1_attn_beta2),
        "router_w": np.asarray(L1_ffn_router_w),
        "router_b": rows(L1_ffn_router_b),
        "expert_w": np.asarray(L1_ffn_expert_w).transpose(1, 0, 2).reshape(C, EXPERTS * C),
        "expert_b": bias_blocks.reshape(BLOCKS * EXPERTS, BLOCKS, C),
        "earlier": np.tile(np.tril(np.ones((EXPERTS, EXPERTS), np.float32), -1)[None], (128, 1, 1)),
    }
    nc = bacc.Bacc("TRN2", target_bir_lowering=False, num_devices=1)
    arrays, args = {}, []
    for name, array in laid_out.items():
        array = np.ascontiguousarray(array)
        arrays[f"in_{name}"] = array
        args.append(nc.dram_tensor(f"in_{name}", array.shape, mybir.dt.from_np(array.dtype), kind="ExternalInput").ap())
    out = nc.dram_tensor("out_image", (IMAGES, C, TOKENS), F32, kind="ExternalOutput").ap()
    conv_hybrid(nc, *args, out)
    result = run_bass_kernel_spmd(nc, [arrays], core_ids=[0])
    return result.results[0]["out_image"].reshape(IMAGES, C, SIDE, SIDE)
```
